# Optimizing a Trainium2 kernel written in Bass

```python
import numpy as np
import jax
import jax.numpy as jnp

def _softmax(x, axis=-1):
    return jax.nn.softmax(x, axis=axis)

def _gelu(x):
    return jax.nn.gelu(x, approximate=True)

def _silu(x):
    return jax.nn.silu(x)

def _sigmoid(x):
    return jax.nn.sigmoid(x)

def _layernorm(x, axis=-1, eps=1e-05):
    m = jnp.mean(x, axis=axis, keepdims=True)
    v = jnp.var(x, axis=axis, keepdims=True)
    return (x - m) / jnp.sqrt(v + eps)

def _scatter_add(tgt, idx, src, axis=0):
    return tgt.at[idx].add(src)

def _segment_sum(src, seg, n):
    return jax.ops.segment_sum(src, seg, n)
kernel_name = 'mk_gnn_preln_d2_gnn_r8_9d28d5'

def setup_inputs(seed: int=0):
    np.random.seed(seed)
    _w = jnp.asarray

    def _rec_inputs():
        import jax
        import jax.numpy as jnp
        _gk = jax.random.key(seed)
        x = -0.0003713 + 1 * jax.random.normal(jax.random.fold_in(_gk, 1), (3125, 512), jnp.float32)
        src = jax.random.randint(jax.random.fold_in(_gk, 2), (50000,), 0, 3125, jnp.int32)
        dst = jax.random.randint(jax.random.fold_in(_gk, 3), (50000,), 0, 3125, jnp.int32)
        _o = jnp.argsort(dst, stable=True)
        src = src[_o]
        dst = dst[_o]
        return (x, src, dst)
    x, src, dst = _rec_inputs()

    def _L0_gnn_setup():
        import jax, jax.numpy as jnp
        import numpy as np
        N = 3125
        E = 50000
        HIDDEN = 512
        NH = 8
        DH = HIDDEN // NH
        key = jax.random.key(seed)
        ks = jax.random.split(key, 10)
        s = 1.0 / np.sqrt(HIDDEN)
        return {'h': jax.random.normal(ks[0], (N, HIDDEN), dtype=jnp.float32), 'Wq': jax.random.normal(ks[1], (HIDDEN, HIDDEN), dtype=jnp.float32) * s, 'bq': jnp.zeros((HIDDEN,), dtype=jnp.float32), 'Wk': jax.random.normal(ks[2], (HIDDEN, HIDDEN), dtype=jnp.float32) * s, 'bk': jnp.zeros((HIDDEN,), dtype=jnp.float32), 'Wo': jax.random.normal(ks[3], (HIDDEN, HIDDEN), dtype=jnp.float32) * s, 'bo': jnp.zeros((HIDDEN,), dtype=jnp.float32), 'rows': jax.random.randint(ks[4], (E,), 0, N, dtype=jnp.int32), 'cols': jax.random.randint(ks[5], (E,), 0, N, dtype=jnp.int32)}
    _L0_gnn_all = _L0_gnn_setup()
    _L0_gnn_in = {k: v for k, v in _L0_gnn_all.items() if k in ('Wq', 'bq', 'Wk', 'bk', 'Wo', 'bo')}
    del _L0_gnn_all

    def _L1_gnn_setup():
        import jax, jax.numpy as jnp
        import numpy as np
        N = 6250
        E = 100000
        F_IN = 512
        F_OUT = 512
        key = jax.random.key(seed)
        k_feat, k_src, k_dst, k_w1, k_b1, k_w2, k_b2 = jax.random.split(key, 7)
        feat = jax.random.normal(k_feat, (N, F_IN), dtype=jnp.float32)
        src_idx = jax.random.randint(k_src, (E,), 0, N, dtype=jnp.int32)
        dst_idx = jax.random.randint(k_dst, (E,), 0, N, dtype=jnp.int32)
        deg = jax.ops.segment_sum(jnp.ones((E,), jnp.float32), dst_idx, num_segments=N)
        in_deg = jnp.maximum(deg, 1.0)
        stdv = 1.0 / np.sqrt(F_IN)
        W1 = jax.random.uniform(k_w1, (F_OUT, F_IN), jnp.float32, -stdv, stdv)
        b1 = jax.random.uniform(k_b1, (F_OUT,), jnp.float32, -stdv, stdv)
        W2 = jax.random.uniform(k_w2, (F_OUT, F_IN), jnp.float32, -stdv, stdv)
        b2 = jax.random.uniform(k_b2, (F_OUT,), jnp.float32, -stdv, stdv)
        return {'feat': feat, 'src_idx': src_idx, 'dst_idx': dst_idx, 'in_deg': in_deg, 'W1': W1, 'b1': b1, 'W2': W2, 'b2': b2}
    _L1_gnn_all = _L1_gnn_setup()
    _L1_gnn_in = {k: v for k, v in _L1_gnn_all.items() if k in ('W1', 'b1', 'W2', 'b2')}
    del _L1_gnn_all
    return {'x': x, 'src': src, 'dst': dst, 'L0_gnn_Wq': _L0_gnn_in['Wq'], 'L0_gnn_bq': _L0_gnn_in['bq'], 'L0_gnn_Wk': _L0_gnn_in['Wk'], 'L0_gnn_bk': _L0_gnn_in['bk'], 'L0_gnn_Wo': _L0_gnn_in['Wo'], 'L0_gnn_bo': _L0_gnn_in['bo'], 'L1_gnn_W1': _L1_gnn_in['W1'], 'L1_gnn_b1': _L1_gnn_in['b1'], 'L1_gnn_W2': _L1_gnn_in['W2'], 'L1_gnn_b2': _L1_gnn_in['b2']}

def reference(x, src, dst, L0_gnn_Wq, L0_gnn_bq, L0_gnn_Wk, L0_gnn_bk, L0_gnn_Wo, L0_gnn_bo, L1_gnn_W1, L1_gnn_b1, L1_gnn_W2, L1_gnn_b2):
    import jax
    import jax.numpy as jnp

    def _L0_gnn_ref(h, Wq, bq, Wk, bk, Wo, bo, rows, cols):
        import jax, jax.numpy as jnp
        import numpy as np
        N = 3125
        E = 50000
        HIDDEN = 512
        NH = 8
        DH = HIDDEN // NH
        q = (h @ Wq + bq).reshape(N, DH, NH)
        k = (h @ Wk + bk).reshape(N, DH, NH)
        v = k
        scores = jnp.einsum('edh,edh->eh', q[rows], k[cols])
        m = jax.ops.segment_max(scores, rows, num_segments=N)
        ex = jnp.exp(scores - m[rows])
        denom = jax.ops.segment_sum(ex, rows, num_segments=N)
        attn = ex / denom[rows]
        msgs = attn[:, None, :] * v[cols]
        out = jax.ops.segment_sum(msgs, rows, num_segments=N)
        return out.reshape(N, HIDDEN) @ Wo + bo

    def _L1_gnn_ref(feat, src_idx, dst_idx, in_deg, W1, b1, W2, b2):
        import jax, jax.numpy as jnp
        import numpy as np
        N = 6250
        E = 100000
        F_IN = 512
        F_OUT = 512
        num_dst = in_deg.shape[0]
        agg = jax.ops.segment_sum(feat[src_idx], dst_idx, num_segments=num_dst)
        ah = agg / in_deg[:, None]
        out = jnp.einsum('nf,of->no', feat[:num_dst], W1) + b1 + jnp.einsum('nf,of->no', ah, W2) + b2
        return out
    deg = jnp.maximum(jax.ops.segment_sum(jnp.ones(dst.shape, jnp.float32), dst, num_segments=3125), 1.0)
    h = jnp.maximum(_layernorm(x, axis=-1), 0.0)
    x = x + _L0_gnn_ref(h, L0_gnn_Wq, L0_gnn_bq, L0_gnn_Wk, L0_gnn_bk, L0_gnn_Wo, L0_gnn_bo, src, dst)
    h = jnp.maximum(_layernorm(x, axis=-1), 0.0)
    x = x + _L1_gnn_ref(h, src, dst, deg, L1_gnn_W1, L1_gnn_b1, L1_gnn_W2, L1_gnn_b2)
    return x

_drawn_inputs = setup_inputs


def setup_inputs(seed=0):
    import zlib

    import numpy as np

    out = dict(_drawn_inputs(seed))
    spreads = {'L0_gnn_bq': (0.0, 0.1), 'L0_gnn_bk': (0.0, 0.1), 'L0_gnn_bo': (0.0, 0.1)}
    factors = {'L1_gnn_b1': 2.871, 'L1_gnn_b2': 2.797}
    for name, (base, spread) in spreads.items():
        noise = np.random.default_rng([zlib.crc32(name.encode()), seed]).standard_normal(out[name].shape)
        drawn = base * np.exp(spread * noise) if base else spread * noise
        out[name] = jnp.asarray(drawn.astype(out[name].dtype))
    for name, factor in factors.items():
        out[name] = (out[name] * factor).astype(out[name].dtype)
    return out
```

```python
def build(nc, io):
    import concourse.bass as bass
    from concourse import mybir
    from contextlib import ExitStack

    F32, BF16, I32 = mybir.dt.float32, mybir.dt.bfloat16, mybir.dt.int32
    ALU, ACT, AX = mybir.AluOpType, mybir.ActivationFunctionType, mybir.AxisListType

    N, D = io["x"].shape
    E = io["src"].shape[0]
    H = 8
    DH = D // H
    WIN = 125
    NW = N // WIN
    EP = 125
    EI = E // EP
    KC = D // 128
    CT = 17
    CAP = 128 * CT
    GMAX = NW + E // CAP
    GMAX += GMAX % 2
    GTAB = GMAX + 2
    SHIFT = 12
    SC = 16
    BIG = 1e30
    EPS = 1e-5
    ROUND = 1.5 * 2.0 ** 23
    SPLIT = 3
    HALF = 1024
    assert N == NW * WIN and E == EP * EI and EI % SC == 0 and NW % 2 == 1 and N < 2 ** SHIFT

    ctx = ExitStack()
    with ctx:
        def sb(name, shape, dt=F32):
            return ctx.enter_context(nc.sbuf_tensor(name, shape, dt))

        def sem(name):
            return ctx.enter_context(nc.semaphore(name))

        def dram(name, shape, dt=F32):
            return nc.dram_tensor(name, shape, dt).ap()

        qtab, ktab, h2tab = dram("qtab", [N, D]), dram("ktab", [N, D]), dram("h2tab", [N, D])
        attn_tab, mean_tab = dram("attn_tab", [N, D]), dram("mean_tab", [N, D])
        sorted_tab = [dram(f"sorted_tab{j}", [E + CAP, 1], I32) for j in range(2)]
        chunk_tab = [dram(f"chunk_tab{j}", [GTAB, 2]) for j in range(2)]

        arena = sb("arena", [128, max(2 * CT * D, NW * EI * 3 // 2 + 2 * GTAB * NW)])
        rows = arena[:, 0:2 * CT * D].rearrange("p (b t d) -> p b t d", b=2, t=CT)
        prefix = arena[0:EP, 0:NW * EI]
        hot = arena[0:EP, NW * EI:NW * EI + NW * EI // 2].bitcast(BF16)
        x_sb = sb("x_sb", [WIN, NW, D])
        w_sb = sb("w_sb", [128, 2, KC, D])
        bias_sb = sb("bias_sb", [WIN, 2, D])
        node = sb("node", [128, 4352])
        nrow = node[0:WIN, 0:1024].rearrange("p (b d) -> p b d", b=2)
        ncol = node[:, 1024:2024].rearrange("p (b c n) -> p b c n", b=2, c=KC)
        nout = node[0:WIN, 2024:4072].rearrange("p (b k d) -> p b k d", b=2, k=2)
        ohT = node[0:WIN, 0:CAP]
        mask = node[0:WIN, CAP:2 * CAP]
        oh = sb("oh", [128, CT, WIN])
        sT = sb("sT", [SPLIT * H, CAP], BF16)
        junk = sb("junk", [128, HALF])
        prod = junk[:, :].rearrange("p (b d) -> p b d", b=2)
        q_win = sb("q_win", [WIN, 2, D])
        acc = sb("acc", [WIN, D])
        win_out = sb("win_out", [WIN, D])
        ends = sb("ends", [EP, 2, EI], I32)
        endf = sb("endf", [EP, 2, EI])
        tmpf = sb("tmpf", [EP, 2, EI])
        pos = sb("pos", [EP, 2, EI], I32)
        stage = sb("stage", [EP, 2, 2, SC], I32)
        stats = sb("stats", [WIN, NW, 6])
        mv = sb("mv", [WIN, NW, 2])
        rstd, shift = sb("rstd", [WIN, NW]), sb("shift", [WIN, NW])
        cnt = sb("cnt", [EP, NW])
        tots = sb("tots", [128, 2, NW])
        small = sb("small", [128, 8, NW])
        SPARE = NW * EI + NW * EI // 2
        grid, grid2 = (arena[:, SPARE + k * GTAB * NW:SPARE + (k + 1) * GTAB * NW].rearrange("p (g w) -> p g w", g=GTAB) for k in range(2))
        chunk_f = sb("chunk_f", [128, 4, GTAB])
        chunk_p = sb("chunk_p", [1, 2, GTAB, 2])
        chunk_i = sb("chunk_i", [1, 2, 3, GTAB], I32)
        pk = sb("pk", [128, 2, CT], I32)
        keyi = sb("keyi", [128, CT], I32)
        idx = sb("idx", [128, 2, CT], I32)
        loc = sb("loc", [128, 2, CT])
        par = sb("par", [128, 2, 2])
        sc = sb("sc", [128, CT, H])
        res = sb("res", [128, CT, H])
        parts = sb("parts", [128, CT, SPLIT * H], BF16)
        ex = sb("ex", [128, CT, H])
        mx = sb("mx", [WIN, H, 2])
        mx_last = sb("mx_last", [WIN, H])
        m_run, m_new, dif, alpha = (sb(n, [WIN, H]) for n in ("m_run", "m_new", "dif", "alpha"))
        den, rden = sb("den", [WIN, H]), sb("rden", [WIN, H])
        ident, identb = sb("ident", [128, 128]), sb("identb", [128, 128], BF16)
        ones, before = sb("ones", [128, 128]), sb("before", [EP, EP])
        sel = sb("sel", [SPLIT * H, H, WIN], BF16)
        iota_i = sb("iota_i", [128, 128], I32)
        iota = sb("iota", [128, 128])
        limit_i, limit = sb("limit_i", [128, E // CAP + 1], I32), sb("limit", [128, E // CAP + 1])
        pad = sb("pad", [128, CT], I32)
        zero = sb("zero", [128, 1])

        wide = [ctx.enter_context(nc.psum_tensor(f"wide{i}", [128, HALF], F32)) for i in range(2)]
        turn = [ctx.enter_context(nc.psum_tensor(f"turn{i}", [128, 512], F32)) for i in range(2)]
        accp = ctx.enter_context(nc.psum_tensor("accp", [128, 512], F32))
        tiny = ctx.enter_context(nc.psum_tensor("tiny", [128, 512], F32))
        mexp = tiny[:, 0:CT * H].rearrange("p (t h) -> p t h", h=H)
        denp = tiny[0:WIN, 256:256 + H]
        degp = tiny[0:WIN, 256:257]
        offp, totp = tiny[0:EP, 0:NW], tiny[:, 64:64 + NW]

        x_in, w_in, bias_in, ends_in = sem("x_in"), sem("w_in"), sem("bias_in"), sem("ends_in")
        w_free = sem("w_free")
        consts = sem("consts")
        pool_step = sem("pool_step")
        step = sem("step")
        cnt_ready, offs_ready = sem("cnt_ready"), sem("offs_ready")
        sort_ready = sem("sort_ready")
        stage_ready = [sem("stage_ready0"), sem("stage_ready1")]
        stage_step = sem("stage_step")
        stage_done = [sem("stage_done0"), sem("stage_done1")]
        pad_done, tabs_done = sem("pad_done"), sem("tabs_done")
        var_ready, std_ready, norm_ready = sem("var_ready"), sem("std_ready"), sem("norm_ready")

        def node_sems(p):
            return {n: sem(f"{p}_{n}") for n in ("row_ready", "row_free", "turn_ready", "turn_free", "col_ready", "col_free",
                                                 "sum_ready", "sum_free", "out_ready", "out_free", "step")}

        s1, s3, s4, s5 = (node_sems(p) for p in ("qk", "wo", "ln2", "fin"))
        store1 = [sem("store1_0"), sem("store1_1")]
        load3 = [sem("load3_0"), sem("load3_1")]
        store4 = [sem("store4_0"), sem("store4_1")]
        load5 = [sem("load5_0"), sem("load5_1")]
        store5 = [sem("store5_0"), sem("store5_1")]

        def chunk_sems(p):
            s = {n: sem(f"{p}_{n}") for n in ("pk_free", "idx_ready", "decode", "rows_free", "oh_free", "oh_ready", "step",
                                              "acc_free", "acc_ready", "out_ready", "out_free")}
            for n in ("pk_in", "rows_in"):
                s[n] = [sem(f"{p}_{n}{b}") for b in range(2)]
            s["store"] = sem(f"{p}_store")
            return s

        at, ag = chunk_sems("at"), chunk_sems("ag")
        q_in = [sem("q_in0"), sem("q_in1")]
        q_free = sem("q_free")
        ohT_turn, ohT_ready, turn_free = sem("ohT_turn"), sem("ohT_ready"), sem("turn_free")
        wide_free, q_ready = sem("wide_free"), sem("q_ready")
        parts_ready, sT_turn, sT_ready, unit_ready = sem("parts_ready"), sem("sT_turn"), sem("sT_ready"), sem("unit_ready")
        m_ready, mexp_ready, dif_ready, exp_ready, msg_ready = (sem(n) for n in ("m_ready", "mexp_ready", "dif_ready", "exp_ready", "msg_ready"))

        G_GROUPS = [(0, 4), (4, 4), (8, 4), (12, 4), (16, 1)]
        S_GROUPS = [(0, 8), (8, 8), (16, 1)]
        TURNS = len(G_GROUPS) + len(S_GROUPS)
        assert TURNS % 2 == 0

        passed = {n: sem(f"{n}_passed") for n in ("sp", "pool", "dve")}

        def hold(eng, name, signal, value):
            eng.wait_ge(signal, value)
            eng.sem_inc(passed[name], 1)

        def pairs(eng, n, body):
            with eng.Fori(0, n // 2) as i:
                for b in range(2):
                    body(i * 2 + b, b, i)
            if n % 2:
                body(n - 1, (n - 1) % 2, n // 2)

        def chunks(eng, count, body):
            with eng.Fori(0, GMAX // 2) as i:
                for b in range(2):
                    with eng.If(i * 2 + b < count):
                        body(i * 2 + b, b, i)

        def chunk_count(eng, j):
            return eng.value_load(chunk_i[0:1, j, 2, 0:1], min_val=NW, max_val=GMAX)

        def chunk_count_after(eng, j):
            eng.wait_ge(sort_ready, j + 1)
            return chunk_count(eng, j)

        block = ctx.enter_context(nc.Block())

        @block.sync
        def _(sp):
            for b in range(2):
                sp.dma_start(ends[:, b, :], io["src" if b == 0 else "dst"].rearrange("(p i) -> p i", i=EI)).then_inc(ends_in, 16)
            sp.dma_start(x_sb[:, :, :], io["x"].rearrange("(t p) d -> p t d", p=WIN)).then_inc(x_in, 16)
            for k, n in enumerate(("Wq", "Wk")):
                sp.dma_start(w_sb[:, k, :, :], io[n].rearrange("(c p) d -> p c d", p=128)).then_inc(w_in, 16)
            for k, n in enumerate(("bq", "bk")):
                sp.dma_start(bias_sb[:, k, :], io[n].partition_broadcast(WIN)).then_inc(bias_in, 16)
            sp.wait_ge(consts, 1)
            for j in range(2):
                sp.dma_start(sorted_tab[j][E:E + CAP, :].rearrange("(p t) o -> p (t o)", p=128), pad[:, :]).then_inc(pad_done, 16)

            def store_qk(t, b, i):
                hold(sp, "sp", s1["out_ready"], t * 2 + 2)
                for k, tab in enumerate((qtab, ktab)):
                    sp.dma_start(tab.rearrange("(t p) d -> t p d", p=WIN)[t, :, :] if isinstance(t, int) else tab[bass.ds(t * WIN, WIN), :],
                                 nout[:, b, k, :]).then_inc(store1[b], 16)
                hold(sp, "sp", store1[b], i * 32 + 32)
                sp.sem_inc(s1["out_free"], 1)
            pairs(sp, NW, store_qk)

            for j in range(2):
                hold(sp, "sp", sort_ready, j + 1)
                sp.dma_start(chunk_tab[j].rearrange("(a g) k -> a g k", a=1), chunk_p[0:1, j, :, :]).then_inc(tabs_done, 16)
            sp.wait_ge(tabs_done, 32)
            sp.wait_ge(pad_done, 32)

            def load_chunk(j, s, g, b, i, q):
                first = sp.value_load(chunk_i[0:1, j, 0, bass.ds(g, 1)], min_val=0, max_val=E)
                hold(sp, "sp", s["pk_free"], g + 1)
                sp.dma_start(pk[:, b, :], sorted_tab[j][bass.ds(first, CAP), :].rearrange("(p t) o -> p (t o)", p=128)).then_inc(s["pk_in"][b], 16)
                sp.dma_start(par[:, b, :], chunk_tab[j][bass.ds(g, 1), :].rearrange("a k -> (a k)").partition_broadcast(128)).then_inc(s["pk_in"][b], 16)
                if q:
                    row = sp.value_load(chunk_i[0:1, j, 1, bass.ds(g, 1)], min_val=0, max_val=N - WIN)
                    hold(sp, "sp", q_free, g + 1)
                    sp.dma_start(q_win[:, b, :], qtab[bass.ds(row, WIN), :]).then_inc(q_in[b], 16)

            def chunk_io(j, s, tab, q):
                count = chunk_count(sp, j)
                load_chunk(j, s, 0, 0, 0, q)

                def one(g, b, i):
                    with sp.If(g + 1 < count):
                        load_chunk(j, s, g + 1, 1 - b, i, q)
                    row = sp.value_load(chunk_i[0:1, j, 1, bass.ds(g, 1)], min_val=0, max_val=N - WIN)
                    hold(sp, "sp", s["out_ready"], g + 1)
                    sp.dma_start(tab[bass.ds(row, WIN), :], win_out[:, :]).then_inc(s["store"], 16)
                    hold(sp, "sp", s["store"], g * 16 + 16)
                    sp.sem_inc(s["out_free"], 1)
                chunks(sp, count, one)

            sp.wait_ge(stage_done[0], 2 * SC * 16 * ((EI // SC + 1) // 2))
            sp.wait_ge(stage_done[1], 2 * SC * 16 * (EI // SC // 2))
            chunk_io(0, at, attn_tab, True)

            sp.dma_start(w_sb[:, 0, :, :], io["Wo"].rearrange("(c p) d -> p c d", p=128)).then_inc(w_in, 16)
            sp.dma_start(bias_sb[:, 0, :], io["bo"].partition_broadcast(WIN)).then_inc(bias_in, 16)

            def load_attn(t, b, i):
                hold(sp, "sp", s3["row_free"], t + 1)
                sp.dma_start(nrow[:, b, :], attn_tab[bass.ds(t * WIN, WIN), :]).then_inc(load3[b], 16)
            pairs(sp, NW, load_attn)

            def store_h2(t, b, i):
                hold(sp, "sp", s4["row_ready"], t + 1)
                sp.dma_start(h2tab[bass.ds(t * WIN, WIN), :], nrow[:, b, :]).then_inc(store4[b], 16)
                hold(sp, "sp", store4[b], i * 16 + 16)
                sp.sem_inc(s4["row_free"], 1)
            pairs(sp, NW, store_h2)
            sp.sem_inc(w_free, 1)

            for k, n in enumerate(("W1T", "W2T")):
                sp.dma_start(w_sb[:, k, :, :], io[n].rearrange("(c p) d -> p c d", p=128)).then_inc(w_in, 16)
            for k, n in enumerate(("b1", "b2")):
                sp.dma_start(bias_sb[:, k, :], io[n].partition_broadcast(WIN)).then_inc(bias_in, 16)

            chunk_io(1, ag, mean_tab, False)

            def load_pair(t):
                for k, tab in enumerate((h2tab, mean_tab)):
                    hold(sp, "sp", s5["row_free"], t * 2 + k + 1)
                    sp.dma_start(nrow[:, k, :], tab[bass.ds(t * WIN, WIN), :]).then_inc(load5[k], 16)

            def fin_io(t, b, i):
                load_pair(t)
            def fin_store(t, b, i):
                hold(sp, "sp", s5["out_ready"], t + 1)
                sp.dma_start(io["out"][bass.ds(t * WIN, WIN), :], nout[:, b, 0, :]).then_inc(store5[b], 16)
                hold(sp, "sp", store5[b], i * 16 + 16)
                sp.sem_inc(s5["out_free"], 1)
            load_pair(0)
            with sp.Fori(0, NW // 2) as i:
                for b in range(2):
                    load_pair(i * 2 + b + 1)
                    fin_store(i * 2 + b, b, i)
            fin_store(NW - 1, 0, NW // 2)

        @block.gpsimd
        def _(gp):
            gp.memset(pad[:, :], (2 ** SHIFT - 1) * 2 ** SHIFT).then_inc(consts, 1)
            gp.memset(ident[:, :], 0.0).then_inc(pool_step, 1)
            gp.memset(ones[:, :], 1.0).then_inc(pool_step, 1)
            gp.memset(before[:, :], 1.0).then_inc(pool_step, 1)
            gp.memset(sel[:, :, :], 0.0).then_inc(pool_step, 1)
            gp.iota(iota_i[:, :], pattern=[[1, 128]], base=0, channel_multiplier=0).then_inc(pool_step, 1)
            gp.iota(limit_i[:, :], pattern=[[CAP, E // CAP + 1]], base=0, channel_multiplier=0).then_inc(pool_step, 1)
            gp.wait_ge(pool_step, 6)
            gp.affine_select(out=ident[:, :], in_=ident[:, :], compare_op=ALU.not_equal, fill=1.0, base=0,
                             pattern=[[-1, 128]], channel_multiplier=1).then_inc(pool_step, 1)
            gp.affine_select(out=before[:, :], in_=before[:, :], compare_op=ALU.is_gt, fill=0.0, base=0,
                             pattern=[[1, EP]], channel_multiplier=-1).then_inc(pool_step, 1)
            for k in range(SPLIT):
                gp.affine_select(out=sel[:, :, :], in_=sel[:, :, :], compare_op=ALU.not_equal, fill=1.0, base=-H * k,
                                 pattern=[[-1, H], [0, WIN]], channel_multiplier=1).then_inc(pool_step, 1)
                gp.wait_ge(pool_step, 9 + k)
            gp.tensor_copy(identb[:, :], ident[:, :]).then_inc(pool_step, 1)
            gp.tensor_copy(iota[:, :], iota_i[:, :]).then_inc(pool_step, 1)
            gp.tensor_copy(limit[:, :], limit_i[:, :]).then_inc(pool_step, 1)
            gp.wait_ge(pool_step, 6 + 2 + SPLIT + 3)
            gp.sem_inc(consts, 1)

            for j in range(2):
                def scatter(t, b, i, j=j):
                    hold(gp, "pool", stage_ready[b], i + 1 + j * ((EI // SC + 1 - b) // 2))
                    for c in range(SC):
                        gp.indirect_dma_start(sorted_tab[j], bass.IndirectOffsetOnAxis(ap=stage[:, b, 0, c:c + 1], axis=0),
                                              stage[:, b, 1, c:c + 1], None).then_inc(stage_done[b], 16)
                pairs(gp, EI // SC, scatter)

            def gather(j, s, tab):
                count = chunk_count(gp, j)

                def one(g, b, i):
                    hold(gp, "pool", s["idx_ready"], g + 1)
                    hold(gp, "pool", s["rows_free"], g + 1)
                    for t in range(CT):
                        gp.indirect_dma_start(rows[:, b, t, :], None, tab,
                                              bass.IndirectOffsetOnAxis(ap=idx[:, b, t:t + 1], axis=0)).then_inc(s["rows_in"][b], 16)
                chunks(gp, count, one)

            for b in range(2):
                gp.wait_ge(store1[b], 32 * ((NW + 1 - b) // 2))
            gp.wait_ge(sort_ready, 2)
            gather(0, at, ktab)
            gp.wait_ge(w_free, 1)
            gather(1, ag, h2tab)

        @block.scalar
        def _(act):
            def norm(ready, first, s):
                act.wait_ge(var_ready, first)
                act.activation(rstd[:, :], rstd[:, :], ACT.Sqrt).then_inc(std_ready, 1)
                act.wait_ge(norm_ready, first)

            def relu(t, b, i, s):
                act.wait_ge(s["row_free"], t + 1)
                act.activation(nrow[:, b, :], x_sb[:, bass.ds(t, 1), :].rearrange("p a d -> p (a d)"), ACT.Relu,
                               bias=shift[:, bass.ds(t, 1)], scale=rstd[:, bass.ds(t, 1)]).then_inc(s["row_ready"], 1)

            def turned(t, b, i, s, ring, n=1):
                act.wait_ge(s["turn_ready"], t + 1)
                act.wait_ge(s["col_free"], t + 1)
                act.activation(ncol[:, b, :, :], turn[b][:, 0:KC * WIN].rearrange("p (c n) -> p c n", c=KC), ACT.Copy).then_inc(s["col_ready"], 1)
                act.wait_ge(s["col_ready"], t + 1)
                act.sem_inc(s["turn_free"], 1)

            norm(var_ready, 1, s1)

            def qk(t, b, i):
                relu(t, b, i, s1)
                turned(t, b, i, s1, 2)
            pairs(act, NW, qk)

            count = chunk_count_after(act, 0)

            def one(g, b, i):
                for n, (t0, k) in enumerate(G_GROUPS):
                    act.wait_ge(ohT_turn, g * len(G_GROUPS) + n + 1)
                    src = turn[n % 2][0:WIN, 0:k * 128]
                    act.activation(ohT[:, t0 * 128:(t0 + k) * 128], src, ACT.Copy).then_inc(ohT_ready, 1)
                    act.activation(mask[:, t0 * 128:(t0 + k) * 128], src, ACT.Copy, bias=-BIG, scale=BIG).then_inc(ohT_ready, 1)
                    act.wait_ge(ohT_ready, g * 2 * len(G_GROUPS) + 2 * n + 2)
                    act.sem_inc(turn_free, 1)
                for n, (t0, k) in enumerate(S_GROUPS):
                    act.wait_ge(sT_turn, g * len(S_GROUPS) + n + 1)
                    src = turn[(len(G_GROUPS) + n) % 2][0:SPLIT * H, 0:k * 64].bitcast(BF16)
                    act.activation(sT[:, t0 * 128:(t0 + k) * 128], src, ACT.Copy).then_inc(sT_ready, 1)
                    act.wait_ge(sT_ready, g * len(S_GROUPS) + n + 1)
                    act.sem_inc(turn_free, 1)
                act.wait_ge(dif_ready, g * 2 + 1)
                act.activation(alpha[:, :], dif[:, :], ACT.Exp).then_inc(exp_ready, 1)
                act.wait_ge(dif_ready, g * 2 + 2)
                act.activation(ex[:, :, :], res[:, :, :], ACT.Exp).then_inc(exp_ready, 1)
            chunks(act, count, one)

            def wo(t, b, i):
                turned(t, b, i, s3, 2)
            pairs(act, NW, wo)
            norm(var_ready, 2, s4)
            pairs(act, NW, lambda t, b, i: relu(t, b, i, s4))

            def fin(t, b, i):
                for k in range(2):
                    act.wait_ge(s5["turn_ready"], t * 2 + k + 1)
                    act.wait_ge(s5["col_free"], t * 2 + k + 1)
                    act.activation(ncol[:, k, :, :], turn[k][:, 0:KC * WIN].rearrange("p (c n) -> p c n", c=KC), ACT.Copy).then_inc(s5["col_ready"], 1)
                    act.wait_ge(s5["col_ready"], t * 2 + k + 1)
                    act.sem_inc(s5["turn_free"], 1)
            pairs(act, NW, fin)

        @block.tensor
        def _(pe):
            for s in (s1, s3, s4, s5):
                pe.sem_inc(s["row_free"], 2)
                pe.sem_inc(s["turn_free"], 2)
                pe.sem_inc(s["col_free"], 2)
                pe.sem_inc(s["sum_free"], 2)
                pe.sem_inc(s["out_free"], 2)
            for s in (at, ag):
                pe.sem_inc(s["pk_free"], 2)
                pe.sem_inc(s["rows_free"], 2)
                pe.sem_inc(s["oh_free"], 1)
                pe.sem_inc(s["acc_free"], 1)
                pe.sem_inc(s["out_free"], 1)
            pe.sem_inc(q_free, 2)
            pe.sem_inc(turn_free, 2)
            pe.sem_inc(wide_free, 2)
            pe.wait_ge(consts, 2)

            def offsets(j):
                pe.wait_ge(cnt_ready, j + 1)
                pe.matmul(offp, before[:, :], cnt[:, :], start=True, stop=True)
                pe.matmul(totp, ones[0:EP, :], cnt[:, :], start=True, stop=True).then_inc(offs_ready, 1)

            def to_cols(t, b, s):
                pe.wait_ge(s["turn_free"], t + 1)
                for c in range(KC):
                    last = pe.transpose(turn[b][:, c * WIN:(c + 1) * WIN], nrow[:, b, c * 128:(c + 1) * 128], ident[0:WIN, 0:WIN])
                last.then_inc(s["turn_ready"], 1)

            def product(out, b, w, start=True, stop=True):
                for c in range(KC):
                    last = pe.matmul(out, ncol[:, b, c, :], w_sb[:, w, c, :], start=start and c == 0, stop=stop and c == KC - 1)
                return last

            offsets(0)
            pe.wait_ge(w_in, 32)

            def qk(t, b, i):
                pe.wait_ge(s1["row_ready"], t + 1)
                to_cols(t, b, s1)
                pe.wait_ge(s1["col_ready"], t + 1)
                pe.wait_ge(s1["sum_free"], t + 1)
                product(wide[b][0:WIN, 0:D], b, 0)
                product(wide[b][0:WIN, D:2 * D], b, 1).then_inc(s1["sum_ready"], 1)
            pairs(pe, NW, qk)
            offsets(1)

            count = chunk_count_after(pe, 0)

            def one(g, b, i):
                pe.wait_ge(at["oh_ready"], g + 1)
                for n, (t0, k) in enumerate(G_GROUPS):
                    pe.wait_ge(turn_free, g * TURNS + n + 1)
                    for t in range(t0, t0 + k):
                        last = pe.transpose(turn[n % 2][0:WIN, (t - t0) * 128:(t - t0 + 1) * 128], oh[:, t, :], ident[:, :])
                    last.then_inc(ohT_turn, 1)
                pe.wait_ge(ohT_ready, g * 2 * len(G_GROUPS) + 2 * len(G_GROUPS))
                pe.wait_ge(q_in[b], i * 16 + 16)
                for t in range(CT):
                    pe.wait_ge(wide_free, g * 2 * CT + t + 1)
                    pe.matmul(wide[t % 2][:, 0:D], ohT[:, t * 128:(t + 1) * 128], q_win[:, b, :], start=True, stop=True).then_inc(q_ready, 1)
                pe.wait_ge(parts_ready, g + 1)
                for n, (t0, k) in enumerate(S_GROUPS):
                    m = len(G_GROUPS) + n
                    pe.wait_ge(turn_free, g * TURNS + m + 1)
                    bank = turn[m % 2][0:SPLIT * H, :].bitcast(BF16)
                    for t in range(t0, t0 + k):
                        last = pe.transpose(bank[:, (t - t0) * 128:(t - t0 + 1) * 128], parts[:, t, :], identb[:, :])
                    last.then_inc(sT_turn, 1)
                pe.sem_inc(q_free, 1)
                pe.wait_ge(sT_ready, g * len(S_GROUPS) + len(S_GROUPS))
                for u in range(2 * H + 1):
                    pe.wait_ge(wide_free, g * 2 * CT + CT + u + 1)
                    out = wide[(CT + u) % 2][0:WIN, :]
                    if u < 2 * H:
                        for c in range(2):
                            last = pe.matmul(out[:, c * 512:(c + 1) * 512], sel[:, u // 2, :],
                                             sT[:, (u % 2) * HALF + c * 512:(u % 2) * HALF + (c + 1) * 512], start=True, stop=True)
                    else:
                        for h in range(H):
                            last = pe.matmul(out[:, h * 128:(h + 1) * 128], sel[:, h, :], sT[:, 2 * HALF:CAP], start=True, stop=True)
                    last.then_inc(unit_ready, 1)
                pe.wait_ge(m_ready, g + 1)
                pe.wait_ge(at["acc_free"], g + 1)
                for t in range(CT):
                    last = pe.matmul(mexp[:, t, :], ohT[:, t * 128:(t + 1) * 128], m_new[:, :], start=True, stop=True)
                last.then_inc(mexp_ready, 1)
                for t in range(CT):
                    pe.wait_ge(msg_ready, g * CT + t + 1)
                    pe.matmul(accp[0:WIN, :], oh[:, t, :], rows[:, b, t, :], start=t == 0, stop=t == CT - 1)
                    last = pe.matmul(denp, oh[:, t, :], ex[:, t, :], start=t == 0, stop=t == CT - 1)
                last.then_inc(at["acc_ready"], 1)
                pe.wait_ge(at["acc_ready"], g + 1)
                pe.sem_inc(at["rows_free"], 1)
                pe.sem_inc(at["oh_free"], 1)
            chunks(pe, count, one)

            pe.wait_ge(w_in, 48)

            def wo(t, b, i):
                pe.wait_ge(load3[b], i * 16 + 16)
                to_cols(t, b, s3)
                pe.wait_ge(s3["col_ready"], t + 1)
                pe.sem_inc(s3["row_free"], 1)
                pe.wait_ge(s3["sum_free"], t + 1)
                product(wide[b][0:WIN, 0:D], b, 0).then_inc(s3["sum_ready"], 1)
            pairs(pe, NW, wo)

            count1 = chunk_count_after(pe, 1)

            def agg(g, b, i):
                pe.wait_ge(ag["oh_ready"], g + 1)
                pe.wait_ge(ag["rows_in"][b], (i + 1) * CT * 16)
                pe.wait_ge(ag["acc_free"], g + 1)
                for t in range(CT):
                    pe.matmul(accp[0:WIN, :], oh[:, t, :], rows[:, b, t, :], start=t == 0, stop=t == CT - 1)
                    last = pe.matmul(degp, oh[:, t, :], ones[:, 0:1], start=t == 0, stop=t == CT - 1)
                last.then_inc(ag["acc_ready"], 1)
                pe.wait_ge(ag["acc_ready"], g + 1)
                pe.sem_inc(ag["rows_free"], 1)
                pe.sem_inc(ag["oh_free"], 1)
            chunks(pe, count1, agg)

            pe.wait_ge(w_in, 80)

            def fin(t, b, i):
                for k in range(2):
                    pe.wait_ge(load5[k], t * 16 + 16)
                    pe.wait_ge(s5["turn_free"], t * 2 + k + 1)
                    for c in range(KC):
                        last = pe.transpose(turn[k][:, c * WIN:(c + 1) * WIN], nrow[:, k, c * 128:(c + 1) * 128], ident[0:WIN, 0:WIN])
                    last.then_inc(s5["turn_ready"], 1)
                for k in range(2):
                    pe.wait_ge(s5["col_ready"], t * 2 + k + 1)
                    pe.sem_inc(s5["row_free"], 1)
                    if k == 0:
                        pe.wait_ge(s5["sum_free"], t + 1)
                    last = product(wide[b][0:WIN, 0:D], k, k, start=k == 0, stop=k == 1)
                last.then_inc(s5["sum_ready"], 1)
                pe.wait_ge(s5["sum_ready"], t + 1)
                pe.sem_inc(s5["col_free"], 2)
            pairs(pe, NW, fin)

        @block.vector
        def _(dve):
            steps = [0]

            def then(ins):
                steps[0] += 1
                ins.then_inc(step, 1)
                dve.wait_ge(step, steps[0])

            def moments(n):
                for t in range(NW):
                    last = dve.bn_aggr(mv[:, t, :], stats[:, t, :])
                then(last)
                dve.tensor_scalar(rstd[:, :], mv[:, :, 1], EPS, None, ALU.add).then_inc(var_ready, 1)
                dve.wait_ge(std_ready, n)
                then(dve.reciprocal(rstd[:, :], rstd[:, :]))
                dve.scalar_tensor_tensor(shift[:, :], mv[:, :, 0], -1.0, rstd[:, :], ALU.mult, ALU.mult).then_inc(norm_ready, 1)

            dve.memset(m_run[:, :], 0.0).then_inc(step, 1)
            dve.memset(den[:, :], 0.0).then_inc(step, 1)
            dve.memset(acc[:, :], 0.0).then_inc(step, 1)
            dve.memset(zero[:, :], 0.0).then_inc(step, 1)
            steps[0] = 4
            dve.wait_ge(step, 4)
            dve.wait_ge(x_in, 16)
            with dve.Fori(0, NW) as t:
                dve.bn_stats(stats[:, bass.ds(t, 1), :].rearrange("p a k -> p (a k)"),
                             x_sb[:, bass.ds(t, 1), :].rearrange("p a d -> p (a d)")).then_inc(s1["step"], 1)
            dve.wait_ge(s1["step"], NW)
            moments(1)

            dve.wait_ge(consts, 2)
            dve.wait_ge(ends_in, 32)
            then(dve.tensor_copy(endf[:, :, :], ends[:, :, :]))
            for j in range(2):
                last = dve.scalar_tensor_tensor(ends[:, j, :], endf[:, j, :], float(2 ** SHIFT), endf[:, 1 - j, :], ALU.mult, ALU.add)
            then(last)

            def sort(j):
                win = tmpf[:, 0, :]
                then(dve.tensor_scalar(win, endf[:, j, :], -float(WIN // 2), 1.0 / WIN, ALU.add, ALU.mult))
                then(dve.tensor_scalar(win, win, ROUND, None, ALU.add))
                then(dve.tensor_scalar(win, win, -ROUND, None, ALU.add))
                for w in range(NW):
                    last = dve.tensor_scalar(hot[:, w * EI:(w + 1) * EI], win, float(w), None, ALU.is_equal)
                then(last)
                then(dve.tensor_tensor_scan(prefix, zero[0:EP, 0:1].to_broadcast([EP, NW * EI]), hot, 0.0, ALU.add, ALU.add))
                upto = prefix.rearrange("p (w i) -> p w i", w=NW)
                then(dve.tensor_copy(small[0:EP, 0, :], upto[:, :, EI - 1]))
                then(dve.tensor_copy(cnt[:, 0:1], small[0:EP, 0, 0:1]))
                dve.tensor_tensor(cnt[:, 1:NW], small[0:EP, 0, 1:NW], small[0:EP, 0, 0:NW - 1], ALU.subtract).then_inc(cnt_ready, 1)
                dve.wait_ge(offs_ready, j + 1)
                tot, end, start, nch, cend, cst = (small[:, k, :] for k in range(1, 7))
                off = small[0:EP, 7, :]
                zrow = zero[:, 0:1].to_broadcast([128, NW])
                then(dve.tensor_copy(tot, totp))
                then(dve.tensor_tensor_scan(end, zrow, tot, 0.0, ALU.add, ALU.add))
                then(dve.tensor_tensor(start, end, tot, ALU.subtract))
                then(dve.tensor_tensor(off, offp, start[0:EP, :], ALU.add))
                then(dve.tensor_tensor(off, off, cnt[:, :], ALU.add))
                then(dve.tensor_tensor(off, off, small[0:EP, 0, :], ALU.subtract))
                then(dve.tensor_scalar(off, off, -1.0, None, ALU.add))
                for w in range(NW):
                    last = dve.scalar_tensor_tensor(upto[:, w, :], upto[:, w, :], off[:, w:w + 1], hot[:, w * EI:(w + 1) * EI], ALU.add, ALU.mult)
                then(last)
                then(dve.tensor_reduce(win, prefix.rearrange("p (w i) -> p i w", w=NW), AX.X, ALU.add))
                then(dve.tensor_copy(pos[:, j, :], win))
                K = E // CAP + 1
                g3 = grid[:, 0:NW, 0:K]
                then(dve.tensor_tensor(g3, tot.unsqueeze(2).to_broadcast([128, NW, K]), limit[:, :].unsqueeze(1).to_broadcast([128, NW, K]), ALU.is_gt))
                then(dve.tensor_reduce(nch, g3, AX.X, ALU.add))
                then(dve.tensor_scalar(nch, nch, 1.0, None, ALU.max))
                then(dve.tensor_tensor_scan(cend, zrow, nch, 0.0, ALU.add, ALU.add))
                then(dve.tensor_tensor(cst, cend, nch, ALU.subtract))
                gs = iota[:, 0:GTAB].unsqueeze(2).to_broadcast([128, GTAB, NW])

                def each(v):
                    return v.unsqueeze(1).to_broadcast([128, GTAB, NW])
                then(dve.tensor_tensor(grid[:, :, :], each(cst), gs, ALU.is_le))
                then(dve.tensor_tensor(grid2[:, :, :], each(cend), gs, ALU.is_gt))
                then(dve.tensor_tensor(grid[:, :, :], grid[:, :, :], grid2[:, :, :], ALU.mult))
                base = small[:, 0, :]
                then(dve.scalar_tensor_tensor(base, cst, -float(CAP), start, ALU.mult, ALU.add))
                then(dve.tensor_tensor(grid2[:, :, :], grid[:, :, :], each(base), ALU.mult))
                then(dve.tensor_reduce(chunk_f[:, 0, :], grid2[:, :, :], AX.X, ALU.add))
                then(dve.scalar_tensor_tensor(chunk_f[:, 0, :], iota[:, 0:GTAB], float(CAP), chunk_f[:, 0, :], ALU.mult, ALU.add))
                then(dve.tensor_scalar(chunk_f[:, 0, :], chunk_f[:, 0, :], float(E), None, ALU.min))
                then(dve.tensor_tensor(grid2[:, :, :], grid[:, :, :], each(iota[:, 0:NW]), ALU.mult))
                then(dve.tensor_reduce(chunk_f[:, 1, :], grid2[:, :, :], AX.X, ALU.add))
                then(dve.tensor_scalar(chunk_f[:, 1, :], chunk_f[:, 1, :], float(WIN), None, ALU.mult))
                then(dve.tensor_tensor(grid2[:, :, :], each(cst), gs, ALU.is_equal))
                then(dve.tensor_reduce(chunk_f[:, 2, :], grid2[:, :, :], AX.X, ALU.add))
                then(dve.tensor_copy(chunk_f[:, 3, :], cend[:, NW - 1:NW].to_broadcast([128, GTAB])))
                for k, f in ((0, 0), (1, 1), (2, 3)):
                    then(dve.tensor_copy(chunk_i[0:1, j, k, :], chunk_f[0:1, f, :]))
                then(dve.tensor_copy(chunk_p[0:1, j, :, 0], chunk_f[0:1, 1, :]))
                scale, plus = ((-2 * BIG, 0.0), (-1.0, 1.0))[j]
                then(dve.tensor_scalar(chunk_p[0:1, j, :, 1], chunk_f[0:1, 2, :], scale, plus, ALU.mult, ALU.add))
                dve.sem_inc(sort_ready, 1)

                def to_stage(t, b, i):
                    uses = j * ((EI // SC + 1 - b) // 2)
                    if j == 0:
                        with dve.If(i > 0):
                            hold(dve, "dve", stage_done[b], i * SC * 16)
                    else:
                        dve.wait_ge(stage_done[b], (i + uses) * SC * 16)
                    dve.tensor_copy(stage[:, b, 0, :], pos[:, j, bass.ds(t * SC, SC)]).then_inc(stage_step, 1)
                    dve.tensor_copy(stage[:, b, 1, :], ends[:, j, bass.ds(t * SC, SC)]).then_inc(stage_step, 1)
                    dve.wait_ge(stage_step, (t + j * (EI // SC)) * 2 + 2)
                    dve.sem_inc(stage_ready[b], 1)
                pairs(dve, EI // SC, to_stage)

            sort(0)

            dve.wait_ge(bias_in, 32)

            def qk(t, b, i):
                dve.wait_ge(s1["sum_ready"], t + 1)
                dve.wait_ge(s1["out_free"], t + 1)
                for k in range(2):
                    dve.tensor_tensor(nout[:, b, k, :], wide[b][0:WIN, k * D:(k + 1) * D], bias_sb[:, k, :], ALU.add).then_inc(s1["out_ready"], 1)
                dve.wait_ge(s1["out_ready"], t * 2 + 2)
                dve.sem_inc(s1["sum_free"], 1)
                dve.sem_inc(s1["col_free"], 1)
                dve.sem_inc(s1["row_free"], 1)
            pairs(dve, NW, qk)
            sort(1)

            def decode(s, g, b, i):
                dve.wait_ge(s["pk_in"][b], i * 32 + 32)
                dve.tensor_scalar(idx[:, b, :], pk[:, b, :], 2 ** SHIFT - 1, None, ALU.bitwise_and).then_inc(s["idx_ready"], 1)
                dve.tensor_scalar(keyi[:, :], pk[:, b, :], SHIFT, None, ALU.logical_shift_right).then_inc(s["decode"], 1)
                dve.wait_ge(s["decode"], g * 2 + 1)
                dve.tensor_scalar(loc[:, b, :], keyi[:, :], par[:, b, 0:1], None, ALU.subtract).then_inc(s["decode"], 1)
                dve.wait_ge(s["decode"], g * 2 + 2)
                dve.wait_ge(s["idx_ready"], g + 1)
                dve.sem_inc(s["pk_free"], 1)

            def one_hot(s, g, b):
                dve.wait_ge(s["oh_free"], g + 1)
                dve.tensor_tensor(oh[:, :, :], iota[:, 0:WIN].unsqueeze(1).to_broadcast([128, CT, WIN]),
                                  loc[:, b, :].unsqueeze(2).to_broadcast([128, CT, WIN]), ALU.is_equal).then_inc(s["oh_ready"], 1)

            def heads(v):
                return v.rearrange("p (d h) -> p d h", h=H)

            def by_head(v, n):
                return v.unsqueeze(1).to_broadcast([n, DH, H])

            class Steps:
                def __init__(self, s, g, k):
                    self.s, self.first, self.k, self.n = s["step"], g * k, k, 0

                def mark(self, ins):
                    self.n += 1
                    ins.then_inc(self.s, 1)

                def then(self, ins):
                    self.mark(ins)
                    hold(dve, "dve", self.s, self.first + self.n)

                def end(self):
                    assert self.n == self.k, (self.n, self.k)

            count = chunk_count(dve, 0)
            decode(at, 0, 0, 0)

            def attend(g, b, i):
                st = Steps(at, g, 2 * CT + 5 + 2 * H + 2 + 5 + 8)
                with dve.If(g + 1 < count):
                    decode(at, g + 1, 1 - b, i + b)
                one_hot(at, g, b)
                dve.wait_ge(at["rows_in"][b], (i + 1) * CT * 16)
                for t in range(CT):
                    dve.wait_ge(q_ready, g * CT + t + 1)
                    st.then(dve.tensor_tensor(prod[:, t % 2, :], wide[t % 2][:, 0:D], rows[:, b, t, :], ALU.mult))
                    dve.sem_inc(wide_free, 1)
                    st.mark(dve.tensor_reduce(sc[:, t, :], prod[:, t % 2, :].rearrange("p (d h) -> p h d", h=H), AX.X, ALU.add))
                dve.wait_ge(at["step"], st.first + st.n)
                st.then(dve.tensor_copy(parts[:, :, 0:H], sc[:, :, :]))
                st.then(dve.tensor_tensor(res[:, :, :], sc[:, :, :], parts[:, :, 0:H], ALU.subtract))
                st.then(dve.tensor_copy(parts[:, :, H:2 * H], res[:, :, :]))
                st.then(dve.tensor_tensor(res[:, :, :], res[:, :, :], parts[:, :, H:2 * H], ALU.subtract))
                st.then(dve.tensor_copy(parts[:, :, 2 * H:3 * H], res[:, :, :]))
                dve.sem_inc(parts_ready, 1)
                for u in range(2 * H + 1):
                    hold(dve, "dve", unit_ready, g * (2 * H + 1) + u + 1)
                    unit = wide[(CT + u) % 2][0:WIN, :]
                    if u < 2 * H:
                        st.then(dve.tensor_tensor_reduce(out=junk[0:WIN, :], in0=unit, in1=mask[:, (u % 2) * HALF:(u % 2 + 1) * HALF], scale=1.0,
                                                         scalar=-3 * BIG, op0=ALU.add, op1=ALU.max, accum_out=mx[:, u // 2, u % 2:u % 2 + 1]))
                    else:
                        st.then(dve.tensor_tensor(junk[0:WIN, :].rearrange("p (h e) -> p h e", h=H), unit.rearrange("p (h e) -> p h e", h=H),
                                                  mask[:, 2 * HALF:CAP].unsqueeze(1).to_broadcast([WIN, H, 128]), ALU.add))
                    dve.sem_inc(wide_free, 1)
                st.then(dve.tensor_reduce(mx_last[:, :], junk[0:WIN, :].rearrange("p (h e) -> p h e", h=H), AX.X, ALU.max))
                st.then(dve.tensor_tensor(dif[:, :], mx[:, :, 0], mx[:, :, 1], ALU.max))
                st.then(dve.tensor_tensor(dif[:, :], dif[:, :], mx_last[:, :], ALU.max))
                st.then(dve.scalar_tensor_tensor(m_new[:, :], m_run[:, :], par[0:WIN, b, 1:2], dif[:, :], ALU.add, ALU.max))
                dve.sem_inc(m_ready, 1)
                st.then(dve.scalar_tensor_tensor(dif[:, :], m_run[:, :], par[0:WIN, b, 1:2], m_new[:, :], ALU.add, ALU.subtract))
                dve.sem_inc(dif_ready, 1)
                st.then(dve.tensor_copy(m_run[:, :], m_new[:, :]))
                dve.wait_ge(mexp_ready, g + 1)
                st.then(dve.tensor_tensor(res[:, :, :], sc[:, :, :], mexp, ALU.subtract))
                dve.sem_inc(dif_ready, 1)
                dve.wait_ge(exp_ready, g * 2 + 2)
                for t in range(CT):
                    dve.tensor_tensor(heads(rows[:, b, t, :]), heads(rows[:, b, t, :]), by_head(ex[:, t, :], 128), ALU.mult).then_inc(msg_ready, 1)
                st.mark(dve.tensor_tensor(heads(acc[:, :]), heads(acc[:, :]), by_head(alpha[:, :], WIN), ALU.mult))
                st.then(dve.tensor_tensor(den[:, :], den[:, :], alpha[:, :], ALU.mult))
                dve.wait_ge(at["acc_ready"], g + 1)
                st.mark(dve.tensor_tensor(acc[:, :], acc[:, :], accp[0:WIN, :], ALU.add))
                st.then(dve.tensor_tensor(den[:, :], den[:, :], denp, ALU.add))
                dve.sem_inc(at["acc_free"], 1)
                st.then(dve.tensor_scalar(rden[:, :], den[:, :], 1e-30, None, ALU.max))
                st.then(dve.reciprocal(rden[:, :], rden[:, :]))
                dve.wait_ge(at["out_free"], g + 1)
                st.then(dve.tensor_tensor(heads(win_out[:, :]), heads(acc[:, :]), by_head(rden[:, :], WIN), ALU.mult))
                dve.sem_inc(at["out_ready"], 1)
                st.end()
            chunks(dve, count, attend)

            dve.wait_ge(bias_in, 48)

            def wo(t, b, i):
                xt = x_sb[:, bass.ds(t, 1), :].rearrange("p a d -> p (a d)")
                dve.wait_ge(s3["sum_ready"], t + 1)
                dve.tensor_tensor(win_out[:, :], wide[b][0:WIN, 0:D], bias_sb[:, 0, :], ALU.add).then_inc(s3["step"], 1)
                dve.wait_ge(s3["step"], t * 3 + 1)
                dve.sem_inc(s3["sum_free"], 1)
                dve.sem_inc(s3["col_free"], 1)
                dve.tensor_tensor(xt, xt, win_out[:, :], ALU.add).then_inc(s3["step"], 1)
                dve.wait_ge(s3["step"], t * 3 + 2)
                dve.bn_stats(stats[:, bass.ds(t, 1), :].rearrange("p a k -> p (a k)"), xt).then_inc(s3["step"], 1)
            pairs(dve, NW, wo)
            dve.wait_ge(s3["step"], NW * 3)
            moments(2)

            then(dve.memset(acc[:, :], 0.0))
            then(dve.memset(den[:, 0:1], 0.0))
            count1 = chunk_count(dve, 1)
            decode(ag, 0, 0, 0)

            def agg(g, b, i):
                st = Steps(ag, g, 7)
                with dve.If(g + 1 < count1):
                    decode(ag, g + 1, 1 - b, i + b)
                one_hot(ag, g, b)
                keep = par[0:WIN, b, 1:2]
                dve.wait_ge(ag["acc_ready"], g + 1)
                st.mark(dve.scalar_tensor_tensor(acc[:, :], acc[:, :], keep, accp[0:WIN, :], ALU.mult, ALU.add))
                st.then(dve.scalar_tensor_tensor(den[:, 0:1], den[:, 0:1], keep, degp, ALU.mult, ALU.add))
                dve.sem_inc(ag["acc_free"], 1)
                st.then(dve.tensor_scalar(rden[:, 0:1], den[:, 0:1], 1.0, None, ALU.max))
                st.then(dve.reciprocal(rden[:, 0:1], rden[:, 0:1]))
                dve.wait_ge(ag["out_free"], g + 1)
                st.then(dve.tensor_scalar(win_out[:, :], acc[:, :], rden[:, 0:1], None, ALU.mult))
                st.mark(dve.tensor_copy(rden[:, 1:2], rden[:, 0:1]))
                st.mark(dve.tensor_copy(rden[:, 2:3], rden[:, 0:1]))
                dve.sem_inc(ag["out_ready"], 1)
                st.end()
            chunks(dve, count1, agg)

            dve.wait_ge(bias_in, 80)
            then(dve.tensor_tensor(bias_sb[:, 0, :], bias_sb[:, 0, :], bias_sb[:, 1, :], ALU.add))

            def fin(t, b, i):
                dve.wait_ge(s5["sum_ready"], t + 1)
                dve.tensor_tensor(win_out[:, :], wide[b][0:WIN, 0:D], bias_sb[:, 0, :], ALU.add).then_inc(s5["step"], 1)
                dve.wait_ge(s5["step"], t + 1)
                dve.sem_inc(s5["sum_free"], 1)
                dve.wait_ge(s5["out_free"], t + 1)
                dve.tensor_tensor(nout[:, b, 0, :], win_out[:, :], x_sb[:, bass.ds(t, 1), :].rearrange("p a d -> p (a d)"), ALU.add).then_inc(s5["out_ready"], 1)
                hold(dve, "dve", s5["out_ready"], t + 1)
            pairs(dve, NW, fin)


def kernel(x, src, dst, L0_gnn_Wq, L0_gnn_bq, L0_gnn_Wk, L0_gnn_bk, L0_gnn_Wo, L0_gnn_bo,
           L1_gnn_W1, L1_gnn_b1, L1_gnn_W2, L1_gnn_b2):
    import numpy as np
    import concourse.bacc as bacc
    from concourse import mybir
    from concourse.bass_utils import run_bass_kernel_spmd

    nc = bacc.Bacc("TRN2", target_bir_lowering=False, num_devices=1)
    arrays = {
        "x": x, "src": src, "dst": dst, "Wq": L0_gnn_Wq, "bq": L0_gnn_bq, "Wk": L0_gnn_Wk, "bk": L0_gnn_bk,
        "Wo": L0_gnn_Wo, "bo": L0_gnn_bo, "W1T": np.asarray(L1_gnn_W1).T, "b1": L1_gnn_b1,
        "W2T": np.asarray(L1_gnn_W2).T, "b2": L1_gnn_b2,
    }
    arrays = {n: np.ascontiguousarray(a) for n, a in arrays.items()}
    io = {n: nc.dram_tensor(n, a.shape, mybir.dt.from_np(a.dtype), kind="ExternalInput").ap() for n, a in arrays.items()}
    io["out"] = nc.dram_tensor("out", arrays["x"].shape, mybir.dt.float32, kind="ExternalOutput").ap()
    build(nc, io)
    r = run_bass_kernel_spmd(nc, [arrays], core_ids=[0])
    return r.results[0]["out"]
```

```python
def build(nc, io):
    import concourse.bass as bass
    from concourse import mybir
    from contextlib import ExitStack

    F32, BF16, I32 = mybir.dt.float32, mybir.dt.bfloat16, mybir.dt.int32
    ALU, ACT, AX = mybir.AluOpType, mybir.ActivationFunctionType, mybir.AxisListType

    N, D = io["x"].shape
    E = io["src"].shape[0]
    H = 8
    DH = D // H
    WIN = 125
    NW = N // WIN
    EP = 125
    EI = E // EP
    KC = D // 128
    CT = 17
    CAP = 128 * CT
    GMAX = NW + E // CAP
    GMAX += GMAX % 2
    GTAB = GMAX + 2
    SHIFT = 12
    SC = 16
    BIG = 1e30
    EPS = 1e-5
    ROUND = 1.5 * 2.0 ** 23
    SPLIT = 3
    HALF = 1024
    assert N == NW * WIN and E == EP * EI and EI % SC == 0 and NW % 2 == 1 and N < 2 ** SHIFT

    ctx = ExitStack()
    with ctx:
        def sb(name, shape, dt=F32):
            return ctx.enter_context(nc.sbuf_tensor(name, shape, dt))

        def sem(name):
            return ctx.enter_context(nc.semaphore(name))

        def dram(name, shape, dt=F32):
            return nc.dram_tensor(name, shape, dt).ap()

        qtab, ktab, h2tab = dram("qtab", [N, SPLIT, D], BF16), dram("ktab", [N, D]), dram("h2tab", [N, D])
        attn_tab, mean_tab = dram("attn_tab", [N, D]), dram("mean_tab", [N, D])
        sorted_tab = [dram(f"sorted_tab{j}", [E + CAP, 1], I32) for j in range(2)]
        chunk_tab = [dram(f"chunk_tab{j}", [GTAB, 2]) for j in range(2)]

        arena = sb("arena", [128, max(2 * CT * D, NW * EI * 3 // 2 + 2 * GTAB * NW)])
        rows = arena[:, 0:2 * CT * D].rearrange("p (b t d) -> p b t d", b=2, t=CT)
        prefix = arena[0:EP, 0:NW * EI]
        hot = arena[0:EP, NW * EI:NW * EI + NW * EI // 2].bitcast(BF16)
        nodes = sb("nodes", [128, NW * D])
        x_sb = nodes[0:WIN, :].rearrange("p (t d) -> p t d", t=NW)
        msgs = nodes[:, 0:CT * D].rearrange("p (t d) -> p t d", t=CT)
        prod = nodes[:, CT * D:CT * D + 3 * 2 * D].rearrange("p (b d) -> p b d", b=3)
        LEFT = CT * D + 3 * 2 * D
        sc, res, ex = (nodes[:, LEFT + k * CT * H:LEFT + (k + 1) * CT * H].rearrange("p (t h) -> p t h", h=H) for k in range(3))
        parts = nodes[:, LEFT + 3 * CT * H:LEFT + 3 * CT * H + CT * SPLIT * H // 2].bitcast(BF16).rearrange("p (t h) -> p t h", t=CT)
        w_sb = sb("w_sb", [128, 2, KC, D])
        node = sb("node", [128, 4352])
        nrow = node[0:WIN, 0:1024].rearrange("p (b d) -> p b d", b=2)
        ncol = node[:, 1024:2024].rearrange("p (b c n) -> p b c n", b=2, c=KC)
        nout = node[0:WIN, 2024:4072].rearrange("p (b k d) -> p b k d", b=2, k=2)
        ohT = node[0:WIN, 0:CAP].bitcast(BF16).rearrange("p (b e) -> p b e", b=2)
        mask = node[0:WIN, CAP:2 * CAP].bitcast(BF16).rearrange("p (b e) -> p b e", b=2)
        oh = sb("oh", [128, 2, CT, WIN])
        sT = sb("sT", [SPLIT * H, CAP], BF16)
        junk = sb("junk", [WIN, 2, HALF])
        q_win = sb("q_win", [WIN, 2, SPLIT, D], BF16)
        q_parts = q_win
        acc = sb("acc", [WIN, D])
        win_out = sb("win_out", [WIN, D])
        bias = (acc, win_out)
        ends = sb("ends", [EP, 2, EI], I32)
        endf = junk[:, 0, 0:2 * EI].rearrange("p (j i) -> p j i", j=2)
        tmpf = junk[:, 1, 0:EI]
        pos = sb("pos", [EP, 2, EI], I32)
        stage = sb("stage", [EP, 2, 2, SC], I32)
        stats = sb("stats", [WIN, NW, 6])
        mv = sb("mv", [WIN, NW, 2])
        rstd, shift = sb("rstd", [WIN, NW]), sb("shift", [WIN, NW])
        cnt = sb("cnt", [EP, NW])
        small = sb("small", [128, 8, NW])
        SPARE = NW * EI + NW * EI // 2
        grid, grid2 = (arena[:, SPARE + k * GTAB * NW:SPARE + (k + 1) * GTAB * NW].rearrange("p (g w) -> p g w", g=GTAB) for k in range(2))
        chunk_f = sb("chunk_f", [128, 4, GTAB])
        chunk_p = sb("chunk_p", [1, 2, GTAB, 2])
        chunk_i = sb("chunk_i", [1, 2, 3, GTAB + 1], I32)
        pk = sb("pk", [128, 2, CT], I32)
        keyi = sb("keyi", [128, CT], I32)
        idx = sb("idx", [128, 2, CT], I32)
        loc = sb("loc", [128, 2, CT])
        par = sb("par", [128, 2, 2])
        first_chunk = sb("first_chunk", [128, 2, 1])
        mx = sb("mx", [WIN, H, 2])
        mx_last = sb("mx_last", [WIN, H])
        m_run, m_new, dif, alpha = (sb(n, [WIN, H]) for n in ("m_run", "m_new", "dif", "alpha"))
        m_parts = sb("m_parts", [WIN, SPLIT, H], BF16)
        m_res = sb("m_res", [WIN, H])
        den, rden = sb("den", [WIN, H]), sb("rden", [WIN, H])
        ident, identb = sb("ident", [128, 128]), sb("identb", [128, 128], BF16)
        ones, before = sb("ones", [128, 128]), sb("before", [EP, EP])
        sel = sb("sel", [SPLIT * H, H, WIN], BF16)
        iota_i = arena[:, 0:128].bitcast(I32)
        iota = sb("iota", [128, 128])
        limit_i, limit = arena[:, 128:128 + E // CAP + 1].bitcast(I32), sb("limit", [128, E // CAP + 1])
        pad = sb("pad", [128, CT], I32)
        zero = sb("zero", [128, 1])

        wide = [ctx.enter_context(nc.psum_tensor(f"wide{i}", [128, HALF], F32)) for i in range(2)]
        turn = [ctx.enter_context(nc.psum_tensor(f"turn{i}", [128, 512], F32)) for i in range(2)]
        accp = ctx.enter_context(nc.psum_tensor("accp", [128, 512], F32))
        tiny = ctx.enter_context(nc.psum_tensor("tiny", [128, 512], F32))
        mexp = tiny[:, 0:CT * H].rearrange("p (t h) -> p t h", h=H)
        denp = tiny[0:WIN, 256:256 + H]
        degp = tiny[0:WIN, 256:257]
        offp, totp = tiny[0:EP, 0:NW], tiny[:, 64:64 + NW]

        x_in, w_in, bias_in, ends_in = sem("x_in"), sem("w_in"), sem("bias_in"), sem("ends_in")
        w_free = sem("w_free")
        consts = sem("consts")
        pool_step = sem("pool_step")
        step = sem("step")
        cnt_ready, offs_ready = sem("cnt_ready"), sem("offs_ready")
        sort_ready = sem("sort_ready")
        stage_ready = [sem("stage_ready0"), sem("stage_ready1")]
        stage_step = sem("stage_step")
        stage_done = [sem("stage_done0"), sem("stage_done1")]
        pad_done, tabs_done = sem("pad_done"), sem("tabs_done")
        var_ready, std_ready, norm_ready = sem("var_ready"), sem("std_ready"), sem("norm_ready")

        def node_sems(p):
            return {n: sem(f"{p}_{n}") for n in ("row_ready", "row_free", "turn_ready", "turn_free", "col_ready", "col_free",
                                                 "sum_ready", "sum_free", "out_ready", "out_free", "step", "q_step")}

        s1, s3, s4, s5 = (node_sems(p) for p in ("qk", "wo", "ln2", "fin"))
        store1 = [sem("store1_0"), sem("store1_1")]
        load3 = [sem("load3_0"), sem("load3_1")]
        store4 = [sem("store4_0"), sem("store4_1")]
        load5 = [sem("load5_0"), sem("load5_1")]
        store5 = [sem("store5_0"), sem("store5_1")]

        def chunk_sems(p):
            s = {n: sem(f"{p}_{n}") for n in ("pk_free", "idx_ready", "decode", "rows_free", "oh_ready", "step",
                                              "acc_free", "acc_ready", "out_ready", "out_free")}
            for n in ("pk_in", "rows_in"):
                s[n] = [sem(f"{p}_{n}{b}") for b in range(2)]
            for n in ("store", "kept", "last_step"):
                s[n] = sem(f"{p}_{n}")
            return s

        at, ag = chunk_sems("at"), chunk_sems("ag")
        q_in = [sem("q_in0"), sem("q_in1")]
        q_free = sem("q_free")
        ohT_turn, ohT_ready, turn_free = sem("ohT_turn"), sem("ohT_ready"), sem("turn_free")
        wide_free, q_ready = sem("wide_free"), sem("q_ready")
        parts_ready, sT_turn, sT_ready, unit_ready = sem("parts_ready"), sem("sT_turn"), sem("sT_ready"), sem("unit_ready")
        m_ready, mexp_ready, dif_ready, alpha_ready, exp_ready, msg_ready = (sem(n) for n in ("m_ready", "mexp_ready", "dif_ready", "alpha_ready", "exp_ready", "msg_ready"))
        res_ready = sem("res_ready")

        G_GROUPS = [(0, 4), (4, 4), (8, 4), (12, 4), (16, 1)]
        S_GROUPS = [(0, 8), (8, 8), (16, 1)]
        Q_GROUPS = [(t, min(2, CT - t)) for t in range(0, CT, 2)]
        M_GROUPS = [(t, min(4, CT - t)) for t in range(0, CT, 4)]
        UNITS = 2 * H + 1
        WIDE = len(Q_GROUPS) + UNITS
        SEG_FIRST = CT - len(Q_GROUPS)
        assert WIDE % 2 == 0
        TURNS = len(G_GROUPS) + len(S_GROUPS)
        assert TURNS % 2 == 0

        passed = {n: sem(f"{n}_passed") for n in ("sp", "pool", "dve")}

        def hold(eng, name, signal, value):
            eng.wait_ge(signal, value)
            eng.sem_inc(passed[name], 1)

        def pairs(eng, n, body):
            with eng.Fori(0, n // 2) as i:
                for b in range(2):
                    body(i * 2 + b, b, i)
            if n % 2:
                body(n - 1, (n - 1) % 2, n // 2)

        def chunks(eng, count, body):
            with eng.Fori(0, GMAX // 2) as i:
                for b in range(2):
                    with eng.If(i * 2 + b < count):
                        body(i * 2 + b, b, i)

        def pipeline(eng, count, full, tail):
            with eng.Fori(0, GMAX // 2) as i:
                for b in range(2):
                    with eng.If(i * 2 + b < count):
                        full(i * 2 + b, b, i)
                    with eng.If(i * 2 + b == count):
                        tail(i * 2 + b, b, i)

        def chunk_count(eng, j):
            return eng.value_load(chunk_i[0:1, j, 2, 1:2], min_val=NW, max_val=GMAX)

        def chunk_count_after(eng, j):
            eng.wait_ge(sort_ready, j + 1)
            return chunk_count(eng, j)

        block = ctx.enter_context(nc.Block())

        @block.sync
        def _(sp):
            for b in range(2):
                sp.dma_start(ends[:, b, :], io["src" if b == 0 else "dst"].rearrange("(p i) -> p i", i=EI)).then_inc(ends_in, 16)
            sp.dma_start(x_sb[:, :, :], io["x"].rearrange("(t p) d -> p t d", p=WIN)).then_inc(x_in, 16)
            for k, n in enumerate(("Wq", "Wk")):
                sp.dma_start(w_sb[:, k, :, :], io[n].rearrange("(c p) d -> p c d", p=128)).then_inc(w_in, 16)
            for k, n in enumerate(("bq", "bk")):
                sp.dma_start(bias[k][:, :], io[n].partition_broadcast(WIN)).then_inc(bias_in, 16)
            sp.wait_ge(consts, 1)
            for j in range(2):
                sp.dma_start(sorted_tab[j][E:E + CAP, :].rearrange("(p t) o -> p (t o)", p=128), pad[:, :]).then_inc(pad_done, 16)

            def store_qk(t, b, i):
                hold(sp, "sp", s1["out_ready"], t * 2 + 2)
                sp.dma_start(qtab[bass.ds(t * WIN, WIN), :, :], q_parts[:, b, :, :]).then_inc(store1[b], 16)
                sp.dma_start(ktab[bass.ds(t * WIN, WIN), :], nout[:, b, 1, :]).then_inc(store1[b], 16)
                hold(sp, "sp", store1[b], i * 32 + 32)
                sp.sem_inc(s1["out_free"], 1)
            pairs(sp, NW, store_qk)

            for j in range(2):
                hold(sp, "sp", sort_ready, j + 1)
                sp.dma_start(chunk_tab[j].rearrange("(a g) k -> a g k", a=1), chunk_p[0:1, j, :, :]).then_inc(tabs_done, 16)
            sp.wait_ge(tabs_done, 32)
            sp.wait_ge(pad_done, 32)

            def load_chunk(j, s, g, b, i, q):
                first = sp.value_load(chunk_i[0:1, j, 0, bass.ds(g + 1, 1)], min_val=0, max_val=E)
                hold(sp, "sp", s["pk_free"], g + 1)
                sp.dma_start(pk[:, b, :], sorted_tab[j][bass.ds(first, CAP), :].rearrange("(p t) o -> p (t o)", p=128)).then_inc(s["pk_in"][b], 16)
                sp.dma_start(par[:, b, :], chunk_tab[j][bass.ds(g, 1), :].rearrange("a k -> (a k)").partition_broadcast(128)).then_inc(s["pk_in"][b], 16)
                if q:
                    row = sp.value_load(chunk_i[0:1, j, 1, bass.ds(g + 1, 1)], min_val=0, max_val=N - WIN)
                    hold(sp, "sp", q_free, g + 1)
                    sp.dma_start(q_win[:, b, :, :], qtab[bass.ds(row, WIN), :, :]).then_inc(q_in[b], 16)

            def store_window(j, s, tab, n, ahead):
                row = sp.value_load(chunk_i[0:1, j, 1, bass.ds(n, 1)], min_val=0, max_val=N - WIN)
                hold(sp, "sp", s["out_ready"], n + ahead)
                sp.dma_start(tab[bass.ds(row, WIN), :], win_out[:, :]).then_inc(s["store"], 16)
                hold(sp, "sp", s["store"], n * 16)
                sp.sem_inc(s["out_free"], 1)

            for b in range(2):
                sp.wait_ge(stage_done[b], SC * 16 * ((EI // SC + 1 - b) // 2))
            count = chunk_count(sp, 0)
            load_chunk(0, at, 0, 0, 0, True)

            def attend(g, b, i):
                load_chunk(0, at, g + 1, 1 - b, i, True)
                with sp.If(g > 0):
                    store_window(0, at, attn_tab, g, 1)

            pipeline(sp, count, attend, lambda g, b, i: store_window(0, at, attn_tab, g, 1))

            sp.dma_start(w_sb[:, 0, :, :], io["Wo"].rearrange("(c p) d -> p c d", p=128)).then_inc(w_in, 16)
            sp.dma_start(bias[0][:, :], io["bo"].partition_broadcast(WIN)).then_inc(bias_in, 16)

            def load_attn(t, b, i):
                hold(sp, "sp", s3["row_free"], t + 1)
                sp.dma_start(nrow[:, b, :], attn_tab[bass.ds(t * WIN, WIN), :]).then_inc(load3[b], 16)
                sp.dma_start(x_sb[:, bass.ds(t, 1), :].rearrange("p a d -> p (a d)"), io["x"][bass.ds(t * WIN, WIN), :]).then_inc(load3[b], 16)
            pairs(sp, NW, load_attn)

            def store_h2(t, b, i):
                hold(sp, "sp", s4["row_ready"], t + 1)
                sp.dma_start(h2tab[bass.ds(t * WIN, WIN), :], nrow[:, b, :]).then_inc(store4[b], 16)
                hold(sp, "sp", store4[b], i * 16 + 16)
                sp.sem_inc(s4["row_free"], 1)
            pairs(sp, NW, store_h2)
            sp.sem_inc(w_free, 1)

            for k, n in enumerate(("W1T", "W2T")):
                sp.dma_start(w_sb[:, k, :, :], io[n].rearrange("(c p) d -> p c d", p=128)).then_inc(w_in, 16)

            for b in range(2):
                sp.wait_ge(stage_done[b], 2 * SC * 16 * ((EI // SC + 1 - b) // 2))
            count1 = chunk_count(sp, 1)
            load_chunk(1, ag, 0, 0, 0, False)

            def aggregate(g, b, i):
                with sp.If(g + 1 < count1):
                    load_chunk(1, ag, g + 1, 1 - b, i, False)
                store_window(1, ag, mean_tab, g + 1, 0)
            chunks(sp, count1, aggregate)

            for k, n in enumerate(("b1", "b2")):
                sp.dma_start(bias[k][:, :], io[n].partition_broadcast(WIN)).then_inc(bias_in, 16)

            def load_pair(t):
                for k, tab in enumerate((h2tab, mean_tab)):
                    hold(sp, "sp", s5["row_free"], t * 2 + k + 1)
                    sp.dma_start(nrow[:, k, :], tab[bass.ds(t * WIN, WIN), :]).then_inc(load5[k], 16)

            def fin_io(t, b, i):
                load_pair(t)
            def fin_store(t, b, i):
                hold(sp, "sp", s5["out_ready"], t + 1)
                sp.dma_start(io["out"][bass.ds(t * WIN, WIN), :], nout[:, b, 0, :]).then_inc(store5[b], 16)
                hold(sp, "sp", store5[b], i * 16 + 16)
                sp.sem_inc(s5["out_free"], 1)
            load_pair(0)
            with sp.Fori(0, NW // 2) as i:
                for b in range(2):
                    load_pair(i * 2 + b + 1)
                    fin_store(i * 2 + b, b, i)
            fin_store(NW - 1, 0, NW // 2)

        @block.gpsimd
        def _(gp):
            gp.memset(pad[:, :], (2 ** SHIFT - 1) * 2 ** SHIFT).then_inc(consts, 1)
            gp.memset(ident[:, :], 0.0).then_inc(pool_step, 1)
            gp.memset(ones[:, :], 1.0).then_inc(pool_step, 1)
            gp.memset(before[:, :], 1.0).then_inc(pool_step, 1)
            gp.memset(sel[:, :, :], 0.0).then_inc(pool_step, 1)
            gp.iota(iota_i[:, :], pattern=[[1, 128]], base=0, channel_multiplier=0).then_inc(pool_step, 1)
            gp.iota(limit_i[:, :], pattern=[[CAP, E // CAP + 1]], base=0, channel_multiplier=0).then_inc(pool_step, 1)
            gp.wait_ge(pool_step, 6)
            gp.affine_select(out=ident[:, :], in_=ident[:, :], compare_op=ALU.not_equal, fill=1.0, base=0,
                             pattern=[[-1, 128]], channel_multiplier=1).then_inc(pool_step, 1)
            gp.affine_select(out=before[:, :], in_=before[:, :], compare_op=ALU.is_gt, fill=0.0, base=0,
                             pattern=[[1, EP]], channel_multiplier=-1).then_inc(pool_step, 1)
            for k in range(SPLIT):
                gp.affine_select(out=sel[:, :, :], in_=sel[:, :, :], compare_op=ALU.not_equal, fill=1.0, base=-H * k,
                                 pattern=[[-1, H], [0, WIN]], channel_multiplier=1).then_inc(pool_step, 1)
                gp.wait_ge(pool_step, 9 + k)
            gp.tensor_copy(identb[:, :], ident[:, :]).then_inc(pool_step, 1)
            gp.tensor_copy(iota[:, :], iota_i[:, :]).then_inc(pool_step, 1)
            gp.tensor_copy(limit[:, :], limit_i[:, :]).then_inc(pool_step, 1)
            gp.wait_ge(pool_step, 6 + 2 + SPLIT + 3)
            gp.sem_inc(consts, 1)

            def scatter(j, t, b, i):
                hold(gp, "pool", stage_ready[b], i + 1 + j * ((EI // SC + 1 - b) // 2))
                for c in range(SC):
                    gp.indirect_dma_start(sorted_tab[j], bass.IndirectOffsetOnAxis(ap=stage[:, b, 0, c:c + 1], axis=0),
                                          stage[:, b, 1, c:c + 1], None).then_inc(stage_done[b], 16)

            def gather(s, tab, g, b):
                hold(gp, "pool", s["idx_ready"], g + 1)
                hold(gp, "pool", s["rows_free"], g + 1)
                for t in range(CT):
                    gp.indirect_dma_start(rows[:, b, t, :], None, tab,
                                          bass.IndirectOffsetOnAxis(ap=idx[:, b, t:t + 1], axis=0)).then_inc(s["rows_in"][b], 16)

            pairs(gp, EI // SC, lambda t, b, i: scatter(0, t, b, i))
            for b in range(2):
                gp.wait_ge(store1[b], 32 * ((NW + 1 - b) // 2))
            gp.wait_ge(sort_ready, 2)
            count = chunk_count(gp, 0)

            def attend(g, b, i):
                gather(at, ktab, g, b)
                with gp.If(g < EI // SC):
                    scatter(1, g, b, i)
            chunks(gp, count, attend)

            gp.wait_ge(w_free, 1)
            count1 = chunk_count(gp, 1)
            chunks(gp, count1, lambda g, b, i: gather(ag, h2tab, g, b))

        @block.scalar
        def _(act):
            def norm(ready, first, s):
                act.wait_ge(var_ready, first)
                act.activation(rstd[:, :], rstd[:, :], ACT.Sqrt).then_inc(std_ready, 1)
                act.wait_ge(norm_ready, first)

            def relu(t, b, i, s):
                act.wait_ge(s["row_free"], t + 1)
                act.activation(nrow[:, b, :], x_sb[:, bass.ds(t, 1), :].rearrange("p a d -> p (a d)"), ACT.Relu,
                               bias=shift[:, bass.ds(t, 1)], scale=rstd[:, bass.ds(t, 1)]).then_inc(s["row_ready"], 1)

            def turned(t, b, i, s, ring, n=1):
                act.wait_ge(s["turn_ready"], t + 1)
                act.wait_ge(s["col_free"], t + 1)
                act.activation(ncol[:, b, :, :], turn[b][:, 0:KC * WIN].rearrange("p (c n) -> p c n", c=KC), ACT.Copy).then_inc(s["col_ready"], 1)
                act.wait_ge(s["col_ready"], t + 1)
                act.sem_inc(s["turn_free"], 1)

            norm(var_ready, 1, s1)

            def qk(t, b, i):
                relu(t, b, i, s1)
                turned(t, b, i, s1, 2)
            pairs(act, NW, qk)

            count = chunk_count_after(act, 0)

            def one(g, b, i):
                for n, (t0, k) in enumerate(G_GROUPS):
                    act.wait_ge(ohT_turn, g * len(G_GROUPS) + n + 1)
                    src = turn[n % 2][0:WIN, 0:k * 128]
                    act.activation(ohT[:, b, t0 * 128:(t0 + k) * 128], src, ACT.Copy).then_inc(ohT_ready, 1)
                    act.activation(mask[:, b, t0 * 128:(t0 + k) * 128], src, ACT.Copy, bias=-BIG, scale=BIG).then_inc(ohT_ready, 1)
                    act.wait_ge(ohT_ready, g * 2 * len(G_GROUPS) + 2 * n + 2)
                    act.sem_inc(turn_free, 1)
                for n, (t0, k) in enumerate(S_GROUPS):
                    act.wait_ge(sT_turn, g * len(S_GROUPS) + n + 1)
                    src = turn[(len(G_GROUPS) + n) % 2][0:SPLIT * H, 0:k * 64].bitcast(BF16)
                    act.activation(sT[:, t0 * 128:(t0 + k) * 128], src, ACT.Copy).then_inc(sT_ready, 1)
                    act.wait_ge(sT_ready, g * len(S_GROUPS) + n + 1)
                    act.sem_inc(turn_free, 1)
                act.wait_ge(dif_ready, g + 1)
                act.activation(alpha[:, :], dif[:, :], ACT.Exp).then_inc(alpha_ready, 1)
                act.wait_ge(res_ready, g + 1)
                act.activation(ex[:, :, :], res[:, :, :], ACT.Exp).then_inc(exp_ready, 1)
            chunks(act, count, one)

            def wo(t, b, i):
                turned(t, b, i, s3, 2)
            pairs(act, NW, wo)
            norm(var_ready, 2, s4)
            pairs(act, NW, lambda t, b, i: relu(t, b, i, s4))

            def fin(t, b, i):
                for k in range(2):
                    act.wait_ge(s5["turn_ready"], t * 2 + k + 1)
                    act.wait_ge(s5["col_free"], t * 2 + k + 1)
                    act.activation(ncol[:, k, :, :], turn[k][:, 0:KC * WIN].rearrange("p (c n) -> p c n", c=KC), ACT.Copy).then_inc(s5["col_ready"], 1)
                    act.wait_ge(s5["col_ready"], t * 2 + k + 1)
                    act.sem_inc(s5["turn_free"], 1)
            pairs(act, NW, fin)

        @block.tensor
        def _(pe):
            for s in (s1, s3, s4, s5):
                pe.sem_inc(s["row_free"], 2)
                pe.sem_inc(s["turn_free"], 2)
                pe.sem_inc(s["col_free"], 2)
                pe.sem_inc(s["sum_free"], 2)
                pe.sem_inc(s["out_free"], 2)
            for s in (at, ag):
                pe.sem_inc(s["pk_free"], 2)
                pe.sem_inc(s["acc_free"], 1)
                pe.sem_inc(s["out_free"], 1)
            pe.sem_inc(at["out_free"], 1)
            pe.sem_inc(at["rows_free"], 1)
            pe.sem_inc(ag["rows_free"], 2)
            pe.sem_inc(q_free, 2)
            pe.sem_inc(turn_free, 2)
            pe.sem_inc(wide_free, 2)
            pe.wait_ge(consts, 2)

            def offsets(j):
                pe.wait_ge(cnt_ready, j + 1)
                pe.matmul(offp, before[:, :], cnt[:, :], start=True, stop=True)
                pe.matmul(totp, ones[0:EP, :], cnt[:, :], start=True, stop=True).then_inc(offs_ready, 1)

            def to_cols(t, b, s):
                pe.wait_ge(s["turn_free"], t + 1)
                for c in range(KC):
                    last = pe.transpose(turn[b][:, c * WIN:(c + 1) * WIN], nrow[:, b, c * 128:(c + 1) * 128], ident[0:WIN, 0:WIN])
                last.then_inc(s["turn_ready"], 1)

            def product(out, b, w, start=True, stop=True):
                for c in range(KC):
                    last = pe.matmul(out, ncol[:, b, c, :], w_sb[:, w, c, :], start=start and c == 0, stop=stop and c == KC - 1)
                return last

            offsets(0)
            pe.wait_ge(w_in, 32)

            def qk(t, b, i):
                pe.wait_ge(s1["row_ready"], t + 1)
                to_cols(t, b, s1)
                pe.wait_ge(s1["col_ready"], t + 1)
                pe.wait_ge(s1["sum_free"], t + 1)
                product(wide[b][0:WIN, 0:D], b, 0)
                product(wide[b][0:WIN, D:2 * D], b, 1).then_inc(s1["sum_ready"], 1)
            pairs(pe, NW, qk)
            offsets(1)

            count = chunk_count_after(pe, 0)

            def add_messages(g, b, t):
                if (t, min(4, CT - t)) in M_GROUPS:
                    pe.wait_ge(msg_ready, g * len(M_GROUPS) + t // 4 + 1)
                if t == 0:
                    pe.wait_ge(at["acc_free"], g + 1)
                pe.matmul(accp[0:WIN, :], oh[:, 1 - b, t, :], msgs[:, t, :], start=t == 0, stop=t == CT - 1)
                last = pe.matmul(denp, oh[:, 1 - b, t, :], ex[:, t, :], start=t == 0, stop=t == CT - 1)
                if t == CT - 1:
                    last.then_inc(at["acc_ready"], 1)

            def attend(g, b, i):
                pe.wait_ge(at["oh_ready"], g + 1)
                for n, (t0, k) in enumerate(G_GROUPS):
                    pe.wait_ge(turn_free, g * TURNS + n + 1)
                    for t in range(t0, t0 + k):
                        last = pe.transpose(turn[n % 2][0:WIN, (t - t0) * 128:(t - t0 + 1) * 128], oh[:, b, t, :], ident[:, :])
                    last.then_inc(ohT_turn, 1)
                for t in range(SEG_FIRST):
                    add_messages(g, b, t)
                pe.wait_ge(ohT_ready, g * 2 * len(G_GROUPS) + 2 * len(G_GROUPS))
                pe.wait_ge(q_in[b], i * 16 + 16)
                for n, (t0, k) in enumerate(Q_GROUPS):
                    pe.wait_ge(wide_free, g * WIDE + n + 1)
                    for t in range(t0, t0 + k):
                        for part in range(SPLIT):
                            last = pe.matmul(wide[n % 2][:, (t - t0) * D:(t - t0 + 1) * D], ohT[:, b, t * 128:(t + 1) * 128],
                                             q_win[:, b, part, :], start=part == 0, stop=part == SPLIT - 1)
                    last.then_inc(q_ready, 1)
                    add_messages(g, b, SEG_FIRST + n)
                pe.wait_ge(parts_ready, g + 1)
                for n, (t0, k) in enumerate(S_GROUPS):
                    m = len(G_GROUPS) + n
                    pe.wait_ge(turn_free, g * TURNS + m + 1)
                    bank = turn[m % 2][0:SPLIT * H, :].bitcast(BF16)
                    for t in range(t0, t0 + k):
                        last = pe.transpose(bank[:, (t - t0) * 128:(t - t0 + 1) * 128], parts[:, t, :], identb[:, :])
                    last.then_inc(sT_turn, 1)
                pe.sem_inc(q_free, 1)
                pe.wait_ge(sT_ready, g * len(S_GROUPS) + len(S_GROUPS))
                for u in range(UNITS):
                    n = len(Q_GROUPS) + u
                    pe.wait_ge(wide_free, g * WIDE + n + 1)
                    out = wide[n % 2][0:WIN, :]
                    if u < 2 * H:
                        for c in range(2):
                            last = pe.matmul(out[:, c * 512:(c + 1) * 512], sel[:, u // 2, :],
                                             sT[:, (u % 2) * HALF + c * 512:(u % 2) * HALF + (c + 1) * 512], start=True, stop=True)
                    else:
                        for h in range(H):
                            last = pe.matmul(out[:, h * 128:(h + 1) * 128], sel[:, h, :], sT[:, 2 * HALF:CAP], start=True, stop=True)
                    last.then_inc(unit_ready, 1)
                pe.wait_ge(m_ready, g + 1)
                for t in range(CT):
                    for part in range(SPLIT):
                        last = pe.matmul(mexp[:, t, :], ohT[:, b, t * 128:(t + 1) * 128], m_parts[:, part, :],
                                         start=part == 0, stop=part == SPLIT - 1)
                last.then_inc(mexp_ready, 1)

            def attend_last(g, b, i):
                for t in range(CT):
                    add_messages(g, b, t)
                pe.wait_ge(q_in[b], i * 16 + 16)
            pipeline(pe, count, attend, attend_last)

            pe.wait_ge(w_in, 48)

            def wo(t, b, i):
                pe.wait_ge(load3[b], i * 32 + 32)
                to_cols(t, b, s3)
                pe.wait_ge(s3["col_ready"], t + 1)
                pe.sem_inc(s3["row_free"], 1)
                pe.wait_ge(s3["sum_free"], t + 1)
                product(wide[b][0:WIN, 0:D], b, 0).then_inc(s3["sum_ready"], 1)
            pairs(pe, NW, wo)

            count1 = chunk_count_after(pe, 1)

            def agg(g, b, i):
                pe.wait_ge(ag["oh_ready"], g + 1)
                pe.wait_ge(ag["rows_in"][b], (i + 1) * CT * 16)
                pe.wait_ge(ag["acc_free"], g + 1)
                for t in range(CT):
                    pe.matmul(accp[0:WIN, :], oh[:, b, t, :], rows[:, b, t, :], start=t == 0, stop=t == CT - 1)
                    last = pe.matmul(degp, oh[:, b, t, :], ones[:, 0:1], start=t == 0, stop=t == CT - 1)
                last.then_inc(ag["acc_ready"], 1)
                pe.wait_ge(ag["acc_ready"], g + 1)
                pe.sem_inc(ag["rows_free"], 1)
            chunks(pe, count1, agg)

            pe.wait_ge(w_in, 80)

            def fin(t, b, i):
                for k in range(2):
                    pe.wait_ge(load5[k], t * 16 + 16)
                    pe.wait_ge(s5["turn_free"], t * 2 + k + 1)
                    for c in range(KC):
                        last = pe.transpose(turn[k][:, c * WIN:(c + 1) * WIN], nrow[:, k, c * 128:(c + 1) * 128], ident[0:WIN, 0:WIN])
                    last.then_inc(s5["turn_ready"], 1)
                for k in range(2):
                    pe.wait_ge(s5["col_ready"], t * 2 + k + 1)
                    pe.sem_inc(s5["row_free"], 1)
                    if k == 0:
                        pe.wait_ge(s5["sum_free"], t + 1)
                    last = product(wide[b][0:WIN, 0:D], k, k, start=k == 0, stop=k == 1)
                last.then_inc(s5["sum_ready"], 1)
                pe.wait_ge(s5["sum_ready"], t + 1)
                pe.sem_inc(s5["col_free"], 2)
            pairs(pe, NW, fin)

        @block.vector
        def _(dve):
            steps = [0]

            def then(ins):
                steps[0] += 1
                ins.then_inc(step, 1)
                dve.wait_ge(step, steps[0])

            def moments(n):
                for t in range(NW):
                    last = dve.bn_aggr(mv[:, t, :], stats[:, t, :])
                then(last)
                dve.tensor_scalar(rstd[:, :], mv[:, :, 1], EPS, None, ALU.add).then_inc(var_ready, 1)
                dve.wait_ge(std_ready, n)
                then(dve.reciprocal(rstd[:, :], rstd[:, :]))
                dve.scalar_tensor_tensor(shift[:, :], mv[:, :, 0], -1.0, rstd[:, :], ALU.mult, ALU.mult).then_inc(norm_ready, 1)

            dve.memset(m_run[:, :], 0.0).then_inc(step, 1)
            dve.memset(den[:, :], 0.0).then_inc(step, 1)
            dve.memset(zero[:, :], 0.0).then_inc(step, 1)
            steps[0] = 3
            dve.wait_ge(step, 3)
            dve.wait_ge(x_in, 16)
            with dve.Fori(0, NW) as t:
                dve.bn_stats(stats[:, bass.ds(t, 1), :].rearrange("p a k -> p (a k)"),
                             x_sb[:, bass.ds(t, 1), :].rearrange("p a d -> p (a d)")).then_inc(s1["step"], 1)
            dve.wait_ge(s1["step"], NW)
            moments(1)

            dve.wait_ge(consts, 2)
            dve.wait_ge(ends_in, 32)
            then(dve.tensor_copy(endf[:, :, :], ends[:, :, :]))
            for j in range(2):
                last = dve.scalar_tensor_tensor(ends[:, j, :], endf[:, j, :], float(2 ** SHIFT), endf[:, 1 - j, :], ALU.mult, ALU.add)
            then(last)

            def sort(j):
                win = tmpf[:, :]
                then(dve.tensor_scalar(win, endf[:, j, :], -float(WIN // 2), 1.0 / WIN, ALU.add, ALU.mult))
                then(dve.tensor_scalar(win, win, ROUND, None, ALU.add))
                then(dve.tensor_scalar(win, win, -ROUND, None, ALU.add))
                for w in range(NW):
                    last = dve.tensor_scalar(hot[:, w * EI:(w + 1) * EI], win, float(w), None, ALU.is_equal)
                then(last)
                then(dve.tensor_tensor_scan(prefix, zero[0:EP, 0:1].to_broadcast([EP, NW * EI]), hot, 0.0, ALU.add, ALU.add))
                upto = prefix.rearrange("p (w i) -> p w i", w=NW)
                then(dve.tensor_copy(small[0:EP, 0, :], upto[:, :, EI - 1]))
                then(dve.tensor_copy(cnt[:, 0:1], small[0:EP, 0, 0:1]))
                dve.tensor_tensor(cnt[:, 1:NW], small[0:EP, 0, 1:NW], small[0:EP, 0, 0:NW - 1], ALU.subtract).then_inc(cnt_ready, 1)
                dve.wait_ge(offs_ready, j + 1)
                tot, end, start, nch, cend, cst = (small[:, k, :] for k in range(1, 7))
                off = small[0:EP, 7, :]
                zrow = zero[:, 0:1].to_broadcast([128, NW])
                then(dve.tensor_copy(tot, totp))
                then(dve.tensor_tensor_scan(end, zrow, tot, 0.0, ALU.add, ALU.add))
                then(dve.tensor_tensor(start, end, tot, ALU.subtract))
                then(dve.tensor_tensor(off, offp, start[0:EP, :], ALU.add))
                then(dve.tensor_tensor(off, off, cnt[:, :], ALU.add))
                then(dve.tensor_tensor(off, off, small[0:EP, 0, :], ALU.subtract))
                then(dve.tensor_scalar(off, off, -1.0, None, ALU.add))
                for w in range(NW):
                    last = dve.scalar_tensor_tensor(upto[:, w, :], upto[:, w, :], off[:, w:w + 1], hot[:, w * EI:(w + 1) * EI], ALU.add, ALU.mult)
                then(last)
                then(dve.tensor_reduce(win, prefix.rearrange("p (w i) -> p i w", w=NW), AX.X, ALU.add))
                then(dve.tensor_copy(pos[:, j, :], win))
                K = E // CAP + 1
                g3 = grid[:, 0:NW, 0:K]
                then(dve.tensor_tensor(g3, tot.unsqueeze(2).to_broadcast([128, NW, K]), limit[:, :].unsqueeze(1).to_broadcast([128, NW, K]), ALU.is_gt))
                then(dve.tensor_reduce(nch, g3, AX.X, ALU.add))
                then(dve.tensor_scalar(nch, nch, 1.0, None, ALU.max))
                then(dve.tensor_tensor_scan(cend, zrow, nch, 0.0, ALU.add, ALU.add))
                then(dve.tensor_tensor(cst, cend, nch, ALU.subtract))
                gs = iota[:, 0:GTAB].unsqueeze(2).to_broadcast([128, GTAB, NW])

                def each(v):
                    return v.unsqueeze(1).to_broadcast([128, GTAB, NW])
                then(dve.tensor_tensor(grid[:, :, :], each(cst), gs, ALU.is_le))
                then(dve.tensor_tensor(grid2[:, :, :], each(cend), gs, ALU.is_gt))
                then(dve.tensor_tensor(grid[:, :, :], grid[:, :, :], grid2[:, :, :], ALU.mult))
                base = small[:, 0, :]
                then(dve.scalar_tensor_tensor(base, cst, -float(CAP), start, ALU.mult, ALU.add))
                then(dve.tensor_tensor(grid2[:, :, :], grid[:, :, :], each(base), ALU.mult))
                then(dve.tensor_reduce(chunk_f[:, 0, :], grid2[:, :, :], AX.X, ALU.add))
                then(dve.scalar_tensor_tensor(chunk_f[:, 0, :], iota[:, 0:GTAB], float(CAP), chunk_f[:, 0, :], ALU.mult, ALU.add))
                then(dve.tensor_scalar(chunk_f[:, 0, :], chunk_f[:, 0, :], float(E), None, ALU.min))
                then(dve.tensor_tensor(grid2[:, :, :], grid[:, :, :], each(iota[:, 0:NW]), ALU.mult))
                then(dve.tensor_reduce(chunk_f[:, 1, :], grid2[:, :, :], AX.X, ALU.add))
                then(dve.tensor_scalar(chunk_f[:, 1, :], chunk_f[:, 1, :], float(WIN), None, ALU.mult))
                then(dve.tensor_tensor(grid2[:, :, :], each(cst), gs, ALU.is_equal))
                then(dve.tensor_reduce(chunk_f[:, 2, :], grid2[:, :, :], AX.X, ALU.add))
                then(dve.tensor_copy(chunk_f[:, 3, :], cend[:, NW - 1:NW].to_broadcast([128, GTAB])))
                for k, f in ((0, 0), (1, 1), (2, 3)):
                    then(dve.tensor_copy(chunk_i[0:1, j, k, 1:GTAB + 1], chunk_f[0:1, f, :]))
                then(dve.tensor_copy(chunk_p[0:1, j, :, 0], chunk_f[0:1, 1, :]))
                scale, plus = ((-2 * BIG, 0.0), (-1.0, 1.0))[j]
                then(dve.tensor_scalar(chunk_p[0:1, j, :, 1], chunk_f[0:1, 2, :], scale, plus, ALU.mult, ALU.add))
                dve.sem_inc(sort_ready, 1)

            def to_stage(j, t, b, i):
                blocks = (EI // SC + 1 - b) // 2
                if j == 0:
                    with dve.If(i > 0):
                        hold(dve, "dve", stage_done[b], i * SC * 16)
                else:
                    hold(dve, "dve", stage_done[b], (i + blocks) * SC * 16)
                first = nc.s_assert_within(t * SC, 0, EI - SC, skip_runtime_bounds_check_because="steps are taken for t < EI // SC only")
                dve.tensor_copy(stage[:, b, 0, :], pos[:, j, bass.ds(first, SC)]).then_inc(stage_step, 1)
                dve.tensor_copy(stage[:, b, 1, :], ends[:, j, bass.ds(first, SC)]).then_inc(stage_step, 1)
                dve.wait_ge(stage_step, (t + j * (EI // SC)) * 2 + 2)
                dve.sem_inc(stage_ready[b], 1)

            sort(0)
            pairs(dve, EI // SC, lambda t, b, i: to_stage(0, t, b, i))

            dve.wait_ge(bias_in, 32)

            class Steps:
                def __init__(self, s, g, k):
                    self.s, self.first, self.k, self.n = s, g * k, k, 0

                def mark(self, ins):
                    self.n += 1
                    ins.then_inc(self.s, 1)
                    return self.n

                def seen(self, n):
                    hold(dve, "dve", self.s, self.first + n)

                def then(self, ins):
                    self.seen(self.mark(ins))

                def end(self):
                    assert self.n == self.k, (self.n, self.k)

            def exact_parts(st, part, value, rest):
                st.then(dve.tensor_copy(part(0), value))
                st.then(dve.tensor_tensor(rest, value, part(0), ALU.subtract))
                st.then(dve.tensor_copy(part(1), rest))
                st.then(dve.tensor_tensor(rest, rest, part(1), ALU.subtract))
                st.then(dve.tensor_copy(part(2), rest))

            def qk(t, b, i):
                dve.wait_ge(s1["sum_ready"], t + 1)
                dve.wait_ge(s1["out_free"], t + 1)
                st = Steps(s1["q_step"], t, 6)
                q = nout[:, b, 0, :]
                st.then(dve.tensor_tensor(q, wide[b][0:WIN, 0:D], bias[0][:, :], ALU.add))
                dve.tensor_tensor(nout[:, b, 1, :], wide[b][0:WIN, D:2 * D], bias[1][:, :], ALU.add).then_inc(s1["out_ready"], 1)
                exact_parts(st, lambda k: q_parts[:, b, k, :], q, q)
                st.end()
                dve.wait_ge(s1["out_ready"], t * 2 + 1)
                dve.sem_inc(s1["out_ready"], 1)
                dve.sem_inc(s1["sum_free"], 1)
                dve.sem_inc(s1["col_free"], 1)
                dve.sem_inc(s1["row_free"], 1)
            pairs(dve, NW, qk)
            sort(1)

            def decode(s, g, b, i):
                dve.wait_ge(s["pk_in"][b], i * 32 + 32)
                dve.tensor_scalar(idx[:, b, :], pk[:, b, :], 2 ** SHIFT - 1, None, ALU.bitwise_and).then_inc(s["idx_ready"], 1)
                dve.tensor_scalar(keyi[:, :], pk[:, b, :], SHIFT, None, ALU.logical_shift_right).then_inc(s["decode"], 1)
                dve.tensor_copy(first_chunk[:, b, :], par[:, b, 1:2]).then_inc(s["decode"], 1)
                dve.wait_ge(s["decode"], g * 3 + 2)
                dve.tensor_scalar(loc[:, b, :], keyi[:, :], par[:, b, 0:1], None, ALU.subtract).then_inc(s["decode"], 1)
                dve.wait_ge(s["decode"], g * 3 + 3)
                dve.wait_ge(s["idx_ready"], g + 1)
                dve.sem_inc(s["pk_free"], 1)

            def one_hot(s, g, b):
                dve.tensor_tensor(oh[:, b, :, :], iota[:, 0:WIN].unsqueeze(1).to_broadcast([128, CT, WIN]),
                                  loc[:, b, :].unsqueeze(2).to_broadcast([128, CT, WIN]), ALU.is_equal).then_inc(s["oh_ready"], 1)

            def heads(v):
                return v.rearrange("p (d h) -> p d h", h=H)

            def by_head(v, n):
                return v.unsqueeze(1).to_broadcast([n, DH, H])

            dve.memset(rows[:, 1, :, :], 0.0).then_inc(step, 1)
            dve.memset(oh[:, 1, :, :], 0.0).then_inc(step, 1)
            dve.memset(ex[:, :, :], 0.0).then_inc(step, 1)
            dve.memset(acc[:, :], 0.0).then_inc(step, 1)
            then(dve.memset(alpha[:, :], 0.0))
            steps[0] += 4
            dve.wait_ge(step, steps[0])
            dve.sem_inc(exp_ready, 1)
            dve.sem_inc(alpha_ready, 1)
            count = chunk_count(dve, 0)
            decode(at, 0, 0, 0)
            one_hot(at, 0, 0)

            def messages(g, b):
                dve.wait_ge(exp_ready, g + 1)
                for t0, k in M_GROUPS:
                    out, k_rows = (v[:, t0:t0 + k, :].rearrange("p t (d h) -> p t d h", h=H) for v in (msgs, rows[:, 1 - b, :, :]))
                    weights = ex[:, t0:t0 + k, :].unsqueeze(2).to_broadcast([128, k, DH, H])
                    dve.tensor_tensor(out, k_rows, weights, ALU.mult).then_inc(msg_ready, 1)
                hold(dve, "dve", msg_ready, g * len(M_GROUPS) + len(M_GROUPS))
                dve.sem_inc(at["rows_free"], 1)

            MERGE = 7

            def merge(st, g):
                dve.wait_ge(alpha_ready, g + 1)
                st.mark(dve.tensor_tensor(heads(acc[:, :]), heads(acc[:, :]), by_head(alpha[:, :], WIN), ALU.mult))
                st.then(dve.tensor_tensor(den[:, :], den[:, :], alpha[:, :], ALU.mult))
                dve.wait_ge(at["acc_ready"], g + 1)
                st.mark(dve.tensor_tensor(den[:, :], den[:, :], denp, ALU.add))
                st.mark(dve.tensor_tensor(acc[:, :], acc[:, :], accp[0:WIN, :], ALU.add))
                st.seen(st.n - 1)
                st.then(dve.tensor_scalar(rden[:, :], den[:, :], 1e-30, None, ALU.max))
                dve.sem_inc(at["acc_free"], 1)
                st.then(dve.reciprocal(rden[:, :], rden[:, :]))

            def window_out(st, g):
                dve.wait_ge(at["out_free"], g + 1)
                st.then(dve.tensor_tensor(heads(win_out[:, :]), heads(acc[:, :]), by_head(rden[:, :], WIN), ALU.mult))
                dve.sem_inc(at["out_ready"], 1)

            def attend(g, b, i):
                st = Steps(at["step"], g, 2 * len(Q_GROUPS) + 5 + UNITS + 3 + 1 + 5 + 1 + MERGE)
                messages(g, b)
                decode(at, g + 1, 1 - b, i + b)
                with dve.If(g < EI // SC):
                    to_stage(1, g, b, i)
                dve.wait_ge(at["rows_in"][b], (i + 1) * CT * 16)
                made, summed = [], []
                for n in range(len(Q_GROUPS) + 1):
                    if n < len(Q_GROUPS):
                        t0, k = Q_GROUPS[n]
                        dve.wait_ge(q_ready, g * len(Q_GROUPS) + n + 1)
                        if n >= 3:
                            st.seen(summed[n - 3])
                        made.append(st.mark(dve.tensor_tensor(prod[:, n % 3, 0:k * D], wide[n % 2][:, 0:k * D],
                                                              rows[:, b, t0:t0 + k, :].rearrange("p t d -> p (t d)"), ALU.mult)))
                    if n > 0:
                        t0, k = Q_GROUPS[n - 1]
                        st.seen(made[n - 1])
                        dve.sem_inc(wide_free, 1)
                        summed.append(st.mark(dve.tensor_reduce(sc[:, t0:t0 + k, :], prod[:, (n - 1) % 3, 0:k * D].rearrange("p (t d h) -> p t h d", t=k, h=H),
                                                                AX.X, ALU.add)))
                st.seen(summed[-1])
                exact_parts(st, lambda k: parts[:, :, k * H:(k + 1) * H], sc[:, :, :], res[:, :, :])
                dve.sem_inc(parts_ready, 1)
                merge(st, g)
                window_out(st, g)
                found = []
                for u in range(UNITS):
                    n = len(Q_GROUPS) + u
                    hold(dve, "dve", unit_ready, g * UNITS + u + 1)
                    unit = wide[n % 2][0:WIN, :]
                    if u < 2 * H:
                        found.append(st.mark(dve.tensor_tensor_reduce(
                            out=junk[:, u % 2, :], in0=unit, in1=mask[:, b, (u % 2) * HALF:(u % 2 + 1) * HALF], scale=1.0,
                            scalar=-3 * BIG, op0=ALU.add, op1=ALU.max, accum_out=mx[:, u // 2, u % 2:u % 2 + 1])))
                    else:
                        found.append(st.mark(dve.tensor_tensor(
                            junk[:, u % 2, :].rearrange("p (h e) -> p h e", h=H), unit.rearrange("p (h e) -> p h e", h=H),
                            mask[:, b, 2 * HALF:CAP].unsqueeze(1).to_broadcast([WIN, H, 128]), ALU.add)))
                    if u > 0:
                        st.seen(found[u - 1])
                        dve.sem_inc(wide_free, 1)
                st.seen(found[-1])
                dve.sem_inc(wide_free, 1)
                st.mark(dve.tensor_reduce(mx_last[:, :], junk[:, (UNITS - 1) % 2, :].rearrange("p (h e) -> p h e", h=H), AX.X, ALU.max))
                st.then(dve.tensor_tensor(dif[:, :], mx[:, :, 0], mx[:, :, 1], ALU.max))
                st.then(dve.tensor_tensor(dif[:, :], dif[:, :], mx_last[:, :], ALU.max))
                st.then(dve.scalar_tensor_tensor(m_new[:, :], m_run[:, :], first_chunk[0:WIN, b, :], dif[:, :], ALU.add, ALU.max))
                exact_parts(st, lambda k: m_parts[:, k, :], m_new[:, :], m_res[:, :])
                dve.sem_inc(m_ready, 1)
                st.then(dve.scalar_tensor_tensor(dif[:, :], m_run[:, :], first_chunk[0:WIN, b, :], m_new[:, :], ALU.add, ALU.subtract))
                dve.sem_inc(dif_ready, 1)
                dve.tensor_copy(m_run[:, :], m_new[:, :]).then_inc(at["kept"], 1)
                one_hot(at, g + 1, 1 - b)
                dve.wait_ge(at["kept"], g + 1)
                dve.wait_ge(mexp_ready, g + 1)
                dve.tensor_tensor(res[:, :, :], sc[:, :, :], mexp, ALU.subtract).then_inc(res_ready, 1)
                st.end()

            def attend_last(g, b, i):
                st = Steps(at["last_step"], 0, MERGE)
                messages(g, b)
                merge(st, g)
                window_out(st, g)
                st.end()
            pipeline(dve, count, attend, attend_last)

            dve.wait_ge(bias_in, 48)

            def wo(t, b, i):
                xt = x_sb[:, bass.ds(t, 1), :].rearrange("p a d -> p (a d)")
                dve.wait_ge(s3["sum_ready"], t + 1)
                dve.tensor_tensor(win_out[:, :], wide[b][0:WIN, 0:D], bias[0][:, :], ALU.add).then_inc(s3["step"], 1)
                dve.wait_ge(s3["step"], t * 3 + 1)
                dve.sem_inc(s3["sum_free"], 1)
                dve.sem_inc(s3["col_free"], 1)
                dve.tensor_tensor(xt, xt, win_out[:, :], ALU.add).then_inc(s3["step"], 1)
                dve.wait_ge(s3["step"], t * 3 + 2)
                dve.bn_stats(stats[:, bass.ds(t, 1), :].rearrange("p a k -> p (a k)"), xt).then_inc(s3["step"], 1)
            pairs(dve, NW, wo)
            dve.wait_ge(s3["step"], NW * 3)
            moments(2)

            then(dve.memset(acc[:, :], 0.0))
            then(dve.memset(den[:, 0:1], 0.0))
            count1 = chunk_count(dve, 1)
            decode(ag, 0, 0, 0)

            def agg(g, b, i):
                st = Steps(ag["step"], g, 7)
                with dve.If(g + 1 < count1):
                    decode(ag, g + 1, 1 - b, i + b)
                one_hot(ag, g, b)
                keep = first_chunk[0:WIN, b, :]
                dve.wait_ge(ag["acc_ready"], g + 1)
                st.mark(dve.scalar_tensor_tensor(acc[:, :], acc[:, :], keep, accp[0:WIN, :], ALU.mult, ALU.add))
                st.then(dve.scalar_tensor_tensor(den[:, 0:1], den[:, 0:1], keep, degp, ALU.mult, ALU.add))
                dve.sem_inc(ag["acc_free"], 1)
                st.then(dve.tensor_scalar(rden[:, 0:1], den[:, 0:1], 1.0, None, ALU.max))
                st.then(dve.reciprocal(rden[:, 0:1], rden[:, 0:1]))
                dve.wait_ge(ag["out_free"], g + 1)
                st.then(dve.tensor_scalar(win_out[:, :], acc[:, :], rden[:, 0:1], None, ALU.mult))
                st.mark(dve.tensor_copy(rden[:, 1:2], rden[:, 0:1]))
                st.mark(dve.tensor_copy(rden[:, 2:3], rden[:, 0:1]))
                dve.sem_inc(ag["out_ready"], 1)
                st.end()
            chunks(dve, count1, agg)

            dve.wait_ge(bias_in, 80)
            then(dve.tensor_tensor(bias[0][:, :], bias[0][:, :], bias[1][:, :], ALU.add))

            def fin(t, b, i):
                dve.wait_ge(s5["sum_ready"], t + 1)
                dve.tensor_tensor(win_out[:, :], wide[b][0:WIN, 0:D], bias[0][:, :], ALU.add).then_inc(s5["step"], 1)
                dve.wait_ge(s5["step"], t + 1)
                dve.sem_inc(s5["sum_free"], 1)
                dve.wait_ge(s5["out_free"], t + 1)
                dve.tensor_tensor(nout[:, b, 0, :], win_out[:, :], x_sb[:, bass.ds(t, 1), :].rearrange("p a d -> p (a d)"), ALU.add).then_inc(s5["out_ready"], 1)
                hold(dve, "dve", s5["out_ready"], t + 1)
            pairs(dve, NW, fin)


def kernel(x, src, dst, L0_gnn_Wq, L0_gnn_bq, L0_gnn_Wk, L0_gnn_bk, L0_gnn_Wo, L0_gnn_bo,
           L1_gnn_W1, L1_gnn_b1, L1_gnn_W2, L1_gnn_b2):
    import numpy as np
    import concourse.bacc as bacc
    from concourse import mybir
    from concourse.bass_utils import run_bass_kernel_spmd

    nc = bacc.Bacc("TRN2", target_bir_lowering=False, num_devices=1)
    arrays = {
        "x": x, "src": src, "dst": dst, "Wq": L0_gnn_Wq, "bq": L0_gnn_bq, "Wk": L0_gnn_Wk, "bk": L0_gnn_bk,
        "Wo": L0_gnn_Wo, "bo": L0_gnn_bo, "W1T": np.asarray(L1_gnn_W1).T, "b1": L1_gnn_b1,
        "W2T": np.asarray(L1_gnn_W2).T, "b2": L1_gnn_b2,
    }
    arrays = {n: np.ascontiguousarray(a) for n, a in arrays.items()}
    io = {n: nc.dram_tensor(n, a.shape, mybir.dt.from_np(a.dtype), kind="ExternalInput").ap() for n, a in arrays.items()}
    io["out"] = nc.dram_tensor("out", arrays["x"].shape, mybir.dt.float32, kind="ExternalOutput").ap()
    build(nc, io)
    r = run_bass_kernel_spmd(nc, [arrays], core_ids=[0])
    return r.results[0]["out"]
```

```python
def build(nc, io):
    import concourse.bass as bass
    from concourse import mybir
    from contextlib import ExitStack

    F32, BF16, I32 = mybir.dt.float32, mybir.dt.bfloat16, mybir.dt.int32
    ALU, ACT, AX = mybir.AluOpType, mybir.ActivationFunctionType, mybir.AxisListType

    N, D = io["x"].shape
    E = io["src"].shape[0]
    H = 8
    DH = D // H
    WIN = 125
    NW = N // WIN
    EP = 125
    EI = E // EP
    KC = D // 128
    CT = 17
    CAP = 128 * CT
    GMAX = NW + E // CAP + 1
    BLOCK = 4
    GMAX += -GMAX % (2 * BLOCK)
    GTAB = GMAX + 2
    LAG = 2
    SHIFT = 12
    SC = 25
    STEPS = EI // SC
    BIG = 1e30
    EPS = 1e-5
    ROUND = 1.5 * 2.0 ** 23
    SPLIT = 3
    HALF = 1024
    assert N == NW * WIN and E == EP * EI and EI % (4 * SC) == 0 and NW % 2 == 1 and STEPS <= NW and N < 2 ** SHIFT

    ctx = ExitStack()
    with ctx:
        def sb(name, shape, dt=F32):
            return ctx.enter_context(nc.sbuf_tensor(name, shape, dt))

        def sem(name):
            return ctx.enter_context(nc.semaphore(name))

        def dram(name, shape, dt=F32):
            return nc.dram_tensor(name, shape, dt).ap()

        qtab, ktab, h2tab = dram("qtab", [N, SPLIT, D], BF16), dram("ktab", [N, D]), dram("h2tab", [N, D])
        attn_tab, mean_tab = dram("attn_tab", [N, D]), dram("mean_tab", [N, D])
        sorted_tab = [dram(f"sorted_tab{j}", [E + CAP, 1], I32) for j in range(2)]
        chunk_tab = [dram(f"chunk_tab{j}", [GTAB, 2]) for j in range(2)]

        arena = sb("arena", [128, max(2 * CT * D, NW * EI * 3 // 2 + 2 * GTAB * NW)])
        rows = arena[:, 0:2 * CT * D].rearrange("p (b t d) -> p b t d", b=2, t=CT)
        prefix = arena[0:EP, 0:NW * EI]
        hot = arena[0:EP, NW * EI:NW * EI + NW * EI // 2].bitcast(BF16)
        nodes = sb("nodes", [128, NW * D])
        x_sb = nodes[0:WIN, :].rearrange("p (t d) -> p t d", t=NW)
        HD, HH = D // 2, H // 2
        sums_in = nodes[:, 0:CT * (D + H)].rearrange("p (t u c) -> p t u c", t=CT, u=2)
        msgs, den_in = sums_in[:, :, :, 0:HD], sums_in[:, :, :, HD:HD + HH]
        prod = nodes[:, CT * (D + H):CT * (D + H) + 3 * 2 * D].rearrange("p (b d) -> p b d", b=3)
        LEFT = CT * (D + H) + 3 * 2 * D
        sc, res, ex = (nodes[:, LEFT + k * CT * H:LEFT + (k + 1) * CT * H].rearrange("p (t h) -> p t h", h=H) for k in range(3))
        parts = nodes[:, LEFT + 3 * CT * H:LEFT + 3 * CT * H + CT * SPLIT * H // 2].bitcast(BF16).rearrange("p (t h) -> p t h", t=CT)
        w_sb = sb("w_sb", [128, 2, KC, D])
        node = sb("node", [128, 4352])
        nrow = node[0:WIN, 0:1024].rearrange("p (b d) -> p b d", b=2)
        ncol = node[:, 1024:2024].rearrange("p (b c n) -> p b c n", b=2, c=KC)
        nout = node[0:WIN, 2024:4072].rearrange("p (b k d) -> p b k d", b=2, k=2)
        ohT = node[0:WIN, 0:CAP].bitcast(BF16).rearrange("p (b e) -> p b e", b=2)
        mask = node[0:WIN, CAP:2 * CAP].bitcast(BF16).rearrange("p (b e) -> p b e", b=2)
        oh = sb("oh", [128, 2, CT, WIN])
        sT = sb("sT", [SPLIT * H, CAP], BF16)
        junk = sb("junk", [128, 2, HALF])
        oh_sum = junk[:, 0, 0:2 * WIN].rearrange("p (b n) -> p b n", b=2)
        q_win = sb("q_win", [WIN, 2, SPLIT, D], BF16)
        q_parts = q_win
        acc = sb("acc", [WIN, D])
        win_out = sb("win_out", [WIN, D])
        bias = (acc, win_out)
        ends = sb("ends", [EP, 2, EI], I32)
        endf = junk[0:EP, 0, 0:2 * EI].rearrange("p (j i) -> p j i", j=2)
        tmpf = junk[0:EP, 1, 0:EI]
        tmpb = junk[0:EP, 1, EI:EI + EI // 2].bitcast(BF16)
        pos = sb("pos", [EP, 2, EI], I32)
        stage = sb("stage", [EP, 2, 2, SC], I32)
        stats = sb("stats", [WIN, NW, 6])
        mv = sb("mv", [WIN, NW, 2])
        rstd, shift = sb("rstd", [WIN, NW]), sb("shift", [WIN, NW])
        cnt = sb("cnt", [EP, NW])
        small = sb("small", [128, 8, NW])
        SPARE = NW * EI + NW * EI // 2
        grid, grid2 = (arena[:, SPARE + k * GTAB * NW:SPARE + (k + 1) * GTAB * NW].rearrange("p (g w) -> p g w", g=GTAB) for k in range(2))
        chunk_f = sb("chunk_f", [128, 4, GTAB])
        chunk_p = sb("chunk_p", [1, 2, GTAB, 2])
        chunk_i = sb("chunk_i", [1, 2, 3, GTAB + LAG], I32)
        pk = sb("pk", [128, 2, CT], I32)
        keyi = sb("keyi", [128, CT], I32)
        idx = sb("idx", [128, 2, CT], I32)
        loc = sb("loc", [128, 2, CT])
        par = sb("par", [128, 2, 2])
        first_chunk = sb("first_chunk", [128, 2, 1])
        mx = sb("mx", [WIN, H, 3])
        m_run, m_new, dif = (sb(n, [WIN, H]) for n in ("m_run", "m_new", "dif"))
        alpha = sb("alpha", [WIN, 2, H])
        m_parts = sb("m_parts", [WIN, SPLIT, H], BF16)
        m_res = sb("m_res", [WIN, H])
        den, rden = sb("den", [WIN, H]), sb("rden", [WIN, H])
        ident, identb = sb("ident", [128, 128]), sb("identb", [128, 128], BF16)
        ones, before = sb("ones", [128, 128]), sb("before", [EP, EP])
        sel = sb("sel", [SPLIT * H, H, WIN], BF16)
        iota_i = arena[:, 0:128].bitcast(I32)
        iota = sb("iota", [128, 128])
        limit_i, limit = arena[:, 128:128 + E // CAP + 1].bitcast(I32), sb("limit", [128, E // CAP + 1])
        pad = sb("pad", [128, CT], I32)
        zero = sb("zero", [128, 1])

        wide = [ctx.enter_context(nc.psum_tensor(f"wide{i}", [128, HALF], F32)) for i in range(2)]
        wide.append(ctx.enter_context(nc.psum_tensor("wide2", [128, HALF], F32)))
        turn = [wide[2][:, i * 512:(i + 1) * 512] for i in range(2)]
        sums = ctx.enter_context(nc.psum_tensor("sums", [128, 1024], F32))
        halves = sums[0:WIN, :].rearrange("p (u c) -> p u c", u=2)[:, :, 0:HD + HH]
        accp, denp = halves[:, :, 0:HD], halves[:, :, HD:HD + HH]
        tiny = sums[:, 512 + HD + HH:1024]
        mexp = tiny[:, 0:CT * H].rearrange("p (t h) -> p t h", h=H)
        aggp = sums[0:WIN, 0:D]
        degp = tiny[0:WIN, 0:1]
        offp, totp = tiny[0:EP, 0:NW], tiny[:, 64:64 + NW]

        x_in, w_in, bias_in, ends_in = sem("x_in"), sem("w_in"), sem("bias_in"), sem("ends_in")
        consts = sem("consts")
        pool_step = sem("pool_step")
        step = sem("step")
        cnt_ready, offs_ready = sem("cnt_ready"), sem("offs_ready")
        sort_ready = sem("sort_ready")
        placed = sem("placed")
        stage_step = sem("stage_step")
        stage_done = [sem("stage_done0"), sem("stage_done1")]
        pad_done, tabs_done = sem("pad_done"), sem("tabs_done")
        var_ready, std_ready, norm_ready = sem("var_ready"), sem("std_ready"), sem("norm_ready")

        def node_sems(p):
            return {n: sem(f"{p}_{n}") for n in ("row_ready", "row_free", "turn_ready", "turn_free", "col_ready", "col_free",
                                                 "sum_ready", "sum_free", "out_ready", "out_free", "step", "q_step")}

        s1, s3, s5 = (node_sems(p) for p in ("qk", "wo", "fin"))
        store1 = [sem("store1_0"), sem("store1_1")]
        load3 = [sem("load3_0"), sem("load3_1")]
        store4 = [sem("store4_0"), sem("store4_1")]
        h2_var, h2_std, h2_rstd, h2_shift, table_in = (sem(n) for n in ("h2_var", "h2_std", "h2_rstd", "h2_shift", "table_in"))
        load5 = [sem("load5_0"), sem("load5_1")]
        store5 = [sem("store5_0"), sem("store5_1")]

        def chunk_sems(p):
            s = {n: sem(f"{p}_{n}") for n in ("pk_free", "idx_ready", "decode", "rows_free", "oh_ready", "step",
                                              "acc_free", "acc_ready", "out_ready", "out_free")}
            for n in ("pk_in", "rows_in"):
                s[n] = [sem(f"{p}_{n}{b}") for b in range(2)]
            for n in ("store", "kept", "last_step"):
                s[n] = sem(f"{p}_{n}")
            return s

        at, ag = chunk_sems("at"), chunk_sems("ag")
        q_in = [sem("q_in0"), sem("q_in1")]
        q_free = sem("q_free")
        ohT_turn, ohT_ready, turn_free = sem("ohT_turn"), sem("ohT_ready"), sem("turn_free")
        wide_free, q_ready = sem("wide_free"), sem("q_ready")
        merged, acc_scaled, tail_ready, act_tail_ready = (sem(n) for n in ("merged", "acc_scaled", "tail_ready", "act_tail_ready"))
        unit_free, act_msg_ready, mask_ready = sem("unit_free"), sem("act_msg_ready"), sem("mask_ready")
        parts_ready, sT_turn, sT_ready, unit_ready = sem("parts_ready"), sem("sT_turn"), sem("sT_ready"), sem("unit_ready")
        m_ready, mexp_ready, dif_ready, alpha_ready, exp_ready, msg_ready = (sem(n) for n in ("m_ready", "mexp_ready", "dif_ready", "alpha_ready", "exp_ready", "msg_ready"))
        res_ready = sem("res_ready")

        G_GROUPS = [(0, 4), (4, 4), (8, 4), (12, 4), (16, 1)]
        S_GROUPS = [(0, 8), (8, 8), (16, 1)]
        Q_GROUPS = [(t, min(2, CT - t)) for t in range(0, CT, 2)]
        MT, MA = 4, 13
        TT = 12
        M_GROUPS = [(t, min(4, MT - t)) for t in range(0, MT, 4)]
        UNITS = 2 * H + 1
        SEG = [0] + [1] * (len(Q_GROUPS) - 1) + [4, 1, 4]
        assert sum(SEG) == CT and CT - SEG[-1] <= MA
        TURNS = len(G_GROUPS) + len(S_GROUPS)
        assert TURNS % 2 == 0

        passed = {n: sem(f"{n}_passed") for n in ("sp", "pool", "dve")}

        def hold(eng, name, signal, value):
            eng.wait_ge(signal, value)
            eng.sem_inc(passed[name], 1)

        def pairs(eng, n, body):
            with eng.Fori(0, n // 2) as i:
                for b in range(2):
                    body(i * 2 + b, b, i)
            if n % 2:
                body(n - 1, (n - 1) % 2, n // 2)

        def ahead(eng, n, depth, first, body):
            for d in range(depth):
                first(d, d % 2, d // 2)

            def both(t, b, i):
                first(t + depth, (b + depth) % 2, i + (b + depth) // 2)
                body(t, b, i)
            pairs(eng, n - depth, both)
            for t in range(n - depth, n):
                body(t, t % 2, t // 2)

        def rounds(eng, bound, body):
            with eng.Fori(0, GMAX // 2 // BLOCK) as o:
                with eng.If(o * (2 * BLOCK) < bound):
                    with eng.Fori(0, BLOCK) as k:
                        body(o * BLOCK + k)

        def chunks(eng, count, body):
            def pair(i):
                for b in range(2):
                    with eng.If(i * 2 + b < count):
                        body(i * 2 + b, b, i)
            rounds(eng, count, pair)

        def pipeline(eng, count, full, tail):
            def pair(i):
                for b in range(2):
                    with eng.If(i * 2 + b < count):
                        full(i * 2 + b, b, i)
                    with eng.If(i * 2 + b == count):
                        tail(i * 2 + b, b, i)
            rounds(eng, count + 1, pair)

        def chunk_count(eng, j):
            return eng.value_load(chunk_i[0:1, j, 2, LAG:LAG + 1], min_val=NW, max_val=GMAX - 1)

        def chunk_count_after(eng, j):
            eng.wait_ge(sort_ready, j + 1)
            return chunk_count(eng, j)

        def heads(v):
            return v.rearrange("p (d h) -> p d h", h=H)

        def by_halves(v):
            return v.rearrange("p u (d h) -> p u d h", h=H)

        block = ctx.enter_context(nc.Block())

        @block.sync
        def _(sp):
            for b in range(2):
                sp.dma_start(ends[:, b, :], io["src" if b == 0 else "dst"].rearrange("(p i) -> p i", i=EI)).then_inc(ends_in, 16)
            sp.dma_start(x_sb[:, :, :], io["x"].rearrange("(t p) d -> p t d", p=WIN)).then_inc(x_in, 16)
            for k, n in enumerate(("Wq", "Wk")):
                sp.dma_start(w_sb[:, k, :, :], io[n].rearrange("(c p) d -> p c d", p=128)).then_inc(w_in, 16)
            for k, n in enumerate(("bq", "bk")):
                sp.dma_start(bias[k][:, :], io[n].partition_broadcast(WIN)).then_inc(bias_in, 16)
            sp.wait_ge(consts, 1)
            for j in range(2):
                sp.dma_start(sorted_tab[j][E:E + CAP, :].rearrange("(p t) o -> p (t o)", p=128), pad[:, :]).then_inc(pad_done, 16)

            def store_qk(t, b, i):
                hold(sp, "sp", s1["out_ready"], t + 1)
                sp.dma_start(qtab[bass.ds(t * WIN, WIN), :, :], q_parts[:, b, :, :]).then_inc(store1[b], 16)
                sp.dma_start(ktab[bass.ds(t * WIN, WIN), :], nout[:, b, 1, :]).then_inc(store1[b], 16)
                hold(sp, "sp", store1[b], i * 32 + 32)
                sp.sem_inc(s1["out_free"], 1)
            pairs(sp, NW, store_qk)

            sp.wait_ge(s1["sum_ready"], NW)
            for k, n in enumerate(("Wo", "W1T")):
                sp.dma_start(w_sb[:, k, :, :], io[n].rearrange("(c p) d -> p c d", p=128)).then_inc(w_in, 16)
            for j in range(2):
                hold(sp, "sp", sort_ready, j + 1)
                sp.dma_start(chunk_tab[j].rearrange("(a g) k -> a g k", a=1), chunk_p[0:1, j, :, :]).then_inc(tabs_done, 16)
            sp.wait_ge(tabs_done, 32)
            sp.wait_ge(pad_done, 32)

            def load_chunk(j, s, g, b, i, q):
                first = sp.value_load(chunk_i[0:1, j, 0, bass.ds(g + LAG, 1)], min_val=0, max_val=E)
                hold(sp, "sp", s["pk_free"], g + 1)
                sp.dma_start(pk[:, b, :], sorted_tab[j][bass.ds(first, CAP), :].rearrange("(p t) o -> p (t o)", p=128)).then_inc(s["pk_in"][b], 16)
                sp.dma_start(par[:, b, :], chunk_tab[j][bass.ds(g, 1), :].rearrange("a k -> (a k)").partition_broadcast(128)).then_inc(s["pk_in"][b], 16)
                if q:
                    row = sp.value_load(chunk_i[0:1, j, 1, bass.ds(g + LAG, 1)], min_val=0, max_val=N - WIN)
                    hold(sp, "sp", q_free, g + 1)
                    sp.dma_start(q_win[:, b, :, :], qtab[bass.ds(row, WIN), :, :]).then_inc(q_in[b], 16)

            def store_window(j, s, tab, n, made, stored):
                row = sp.value_load(chunk_i[0:1, j, 1, bass.ds(n, 1)], min_val=0, max_val=N - WIN)
                hold(sp, "sp", s["out_ready"], made)
                sp.dma_start(tab[bass.ds(row, WIN), :], win_out[:, :]).then_inc(s["store"], 16)
                hold(sp, "sp", s["store"], stored * 16)
                sp.sem_inc(s["out_free"], 1)

            for b in range(2):
                sp.wait_ge(stage_done[b], SC * 16 * (STEPS // 2))
            count = chunk_count(sp, 0)
            load_chunk(0, at, 0, 0, 0, True)

            def attend(g, b, i):
                load_chunk(0, at, g + 1, 1 - b, i, True)
                with sp.If(g >= LAG):
                    store_window(0, at, attn_tab, g, g + 1, g + 1)

            def attend_last(g, b, i):
                for n in range(LAG):
                    store_window(0, at, attn_tab, g + n, g + n + 1, g + n + 1)
            sp.sem_inc(at["store"], LAG * 16)
            pipeline(sp, count, attend, attend_last)

            sp.dma_start(bias[0][:, :], io["bo"].partition_broadcast(WIN)).then_inc(bias_in, 16)

            for b in range(2):
                sp.wait_ge(stage_done[b], 2 * SC * 16 * (STEPS // 2))
            count1 = chunk_count(sp, 1)
            for b in range(2):
                load_chunk(1, ag, b, b, 0, False)

            def load_attn(t, b, i):
                hold(sp, "sp", s3["row_free"], t + 1)
                sp.dma_start(nrow[:, b, :], attn_tab[bass.ds(t * WIN, WIN), :]).then_inc(load3[b], 16)
                sp.dma_start(x_sb[:, bass.ds(t, 1), :].rearrange("p a d -> p (a d)"), io["x"][bass.ds(t * WIN, WIN), :]).then_inc(load3[b], 16)

            pairs(sp, NW, load_attn)

            sp.wait_ge(s3["sum_ready"], NW)
            sp.dma_start(w_sb[:, 0, :, :], io["W2T"].rearrange("(c p) d -> p c d", p=128)).then_inc(w_in, 16)

            def aggregate(g, b, i):
                with sp.If(g + 2 < count1):
                    load_chunk(1, ag, g + 2, b, i + 1, False)
                store_window(1, ag, mean_tab, g + LAG, g + 1, g + 1)
            chunks(sp, count1, aggregate)

            for k, n in enumerate(("b1", "b2")):
                sp.dma_start(bias[k][:, :], io[n].partition_broadcast(WIN)).then_inc(bias_in, 16)

            def load_pair(t, b, i):
                hold(sp, "sp", s5["row_free"], t + 1)
                for dst, tab in ((nrow[:, b, :], h2tab), (nout[:, b, 1, :], mean_tab)):
                    sp.dma_start(dst, tab[bass.ds(t * WIN, WIN), :]).then_inc(load5[b], 16)

            def store_out(t, b, i):
                hold(sp, "sp", s5["out_ready"], t + 1)
                sp.dma_start(io["out"][bass.ds(t * WIN, WIN), :], nout[:, b, 0, :]).then_inc(store5[b], 16)
                hold(sp, "sp", store5[b], i * 16 + 16)
                sp.sem_inc(s5["out_free"], 1)
            ahead(sp, NW, 2, load_pair, store_out)

        @block.gpsimd
        def _(gp):
            gp.memset(pad[:, :], (2 ** SHIFT - 1) * 2 ** SHIFT).then_inc(consts, 1)
            gp.memset(ident[:, :], 0.0).then_inc(pool_step, 1)
            gp.memset(ones[:, :], 1.0).then_inc(pool_step, 1)
            gp.memset(before[:, :], 1.0).then_inc(pool_step, 1)
            gp.memset(sel[:, :, :], 0.0).then_inc(pool_step, 1)
            gp.iota(iota_i[:, :], pattern=[[1, 128]], base=0, channel_multiplier=0).then_inc(pool_step, 1)
            gp.iota(limit_i[:, :], pattern=[[CAP, E // CAP + 1]], base=0, channel_multiplier=0).then_inc(pool_step, 1)
            gp.wait_ge(pool_step, 6)
            gp.affine_select(out=ident[:, :], in_=ident[:, :], compare_op=ALU.not_equal, fill=1.0, base=0,
                             pattern=[[-1, 128]], channel_multiplier=1).then_inc(pool_step, 1)
            gp.affine_select(out=before[:, :], in_=before[:, :], compare_op=ALU.is_gt, fill=0.0, base=0,
                             pattern=[[1, EP]], channel_multiplier=-1).then_inc(pool_step, 1)
            for k in range(SPLIT):
                gp.affine_select(out=sel[:, :, :], in_=sel[:, :, :], compare_op=ALU.not_equal, fill=1.0, base=-H * k,
                                 pattern=[[-1, H], [0, WIN]], channel_multiplier=1).then_inc(pool_step, 1)
                gp.wait_ge(pool_step, 9 + k)
            gp.tensor_copy(identb[:, :], ident[:, :]).then_inc(pool_step, 1)
            gp.tensor_copy(iota[:, :], iota_i[:, :]).then_inc(pool_step, 1)
            gp.tensor_copy(limit[:, :], limit_i[:, :]).then_inc(pool_step, 1)
            gp.wait_ge(pool_step, 6 + 2 + SPLIT + 3)
            gp.sem_inc(consts, 1)

            def scatter(j, t, b, i):
                if j == 0:
                    with gp.If(i > 0):
                        hold(gp, "pool", stage_done[b], i * SC * 16)
                else:
                    hold(gp, "pool", stage_done[b], (i + STEPS // 2) * SC * 16)
                first = nc.s_assert_within(t * SC, 0, EI - SC, skip_runtime_bounds_check_because="steps are taken for t < STEPS only")
                gp.tensor_copy(stage[:, b, 0, :], pos[:, j, bass.ds(first, SC)]).then_inc(stage_step, 1)
                gp.tensor_copy(stage[:, b, 1, :], ends[:, j, bass.ds(first, SC)]).then_inc(stage_step, 1)
                hold(gp, "pool", stage_step, (t + j * STEPS) * 2 + 2)
                for c in range(SC):
                    gp.indirect_dma_start(sorted_tab[j], bass.IndirectOffsetOnAxis(ap=stage[:, b, 0, c:c + 1], axis=0),
                                          stage[:, b, 1, c:c + 1], None).then_inc(stage_done[b], 16)

            def gather(s, tab, g, b):
                hold(gp, "pool", s["idx_ready"], g + 1)
                hold(gp, "pool", s["rows_free"], g * 2 + 2)
                for t in range(CT):
                    gp.indirect_dma_start(rows[:, b, t, :], None, tab,
                                          bass.IndirectOffsetOnAxis(ap=idx[:, b, t:t + 1], axis=0)).then_inc(s["rows_in"][b], 16)

            for half in range(2):
                gp.wait_ge(placed, half + 1)
                with gp.Fori(half * STEPS // 4, (half + 1) * STEPS // 4) as i:
                    for b in range(2):
                        scatter(0, i * 2 + b, b, i)
            gp.wait_ge(placed, 4)
            for b in range(2):
                gp.wait_ge(store1[b], 32 * ((NW + 1 - b) // 2))
            gp.wait_ge(sort_ready, 2)
            count = chunk_count(gp, 0)

            gather(at, ktab, 0, 0)

            def attend(g, b, i):
                with gp.If(g + 1 < count):
                    gather(at, ktab, g + 1, 1 - b)
                with gp.If(g < STEPS):
                    scatter(1, g, b, i)
            chunks(gp, count, attend)


            def store_h2(t, b, i):
                hold(gp, "pool", s3["out_ready"], t + 1)
                gp.dma_start(h2tab[bass.ds(t * WIN, WIN), :], nout[:, b, 0, :]).then_inc(store4[b], 16)

            def stored_h2(t, b, i):
                hold(gp, "pool", store4[b], i * 16 + 16)
                gp.sem_inc(s3["out_free"], 1)
            ahead(gp, NW, 1, store_h2, stored_h2)

            count1 = chunk_count(gp, 1)
            chunks(gp, count1, lambda g, b, i: gather(ag, h2tab, g, b))

        @block.scalar
        def _(act):
            def norm(ready, first, s):
                act.wait_ge(var_ready, first)
                act.activation(rstd[:, :], rstd[:, :], ACT.Sqrt).then_inc(std_ready, 1)
                act.wait_ge(norm_ready, first)

            def relu(t, b, i, s):
                act.activation(nrow[:, b, :], x_sb[:, bass.ds(t, 1), :].rearrange("p a d -> p (a d)"), ACT.Relu,
                               bias=shift[:, bass.ds(t, 1)], scale=rstd[:, bass.ds(t, 1)]).then_inc(s["row_ready"], 1)

            def turned(t, b, i, s, ring, n=1):
                act.wait_ge(s["turn_ready"], t + 1)
                act.activation(ncol[:, b, :, :], turn[b][:, 0:KC * WIN].rearrange("p (c n) -> p c n", c=KC), ACT.Copy).then_inc(s["col_ready"], 1)
                act.wait_ge(s["col_ready"], t + 1)
                act.sem_inc(s["turn_free"], 1)

            norm(var_ready, 1, s1)

            ahead(act, NW, 1, lambda t, b, i: (relu(t, b, i, s1), turned(t, b, i, s1, 2)), lambda t, b, i: None)

            count = chunk_count_after(act, 0)

            def messages(g, b, t0, t1, ready):
                act.wait_ge(exp_ready, g + 1)
                for t in range(t0, t1):
                    for h in range(H):
                        last = act.activation(by_halves(msgs[:, t, :, :])[:, :, :, h], by_halves(rows[:, 1 - b, t, :].rearrange("p (u c) -> p u c", u=2))[:, :, :, h],
                                              ACT.Copy, scale=ex[:, t, h:h + 1])
                    last.then_inc(ready, 1)

            def window_out(n, b):
                act.wait_ge(merged, n + 1)
                act.wait_ge(at["out_free"], n + 1)
                for h in range(H):
                    last = act.activation(heads(win_out[:, :])[:, :, h], heads(acc[:, :])[:, :, h], ACT.Copy, scale=rden[:, h:h + 1])
                last.then_inc(at["out_ready"], 1)

            def scale_sums(g, b):
                act.wait_ge(at["out_ready"], g + 1)
                for h in range(H):
                    last = act.activation(heads(acc[:, :])[:, :, h], heads(acc[:, :])[:, :, h], ACT.Copy, scale=alpha[:, 1 - b, h:h + 1])
                last.then_inc(acc_scaled, 1)

            def weights(g, b):
                act.wait_ge(dif_ready, g + 1)
                act.activation(alpha[:, 1 - b, :], dif[:, :], ACT.Exp).then_inc(alpha_ready, 1)
                act.wait_ge(res_ready, g + 1)
                act.activation(ex[:, :, :], res[:, :, :], ACT.Exp)
                act.activation(den_in, res[:, :, :].rearrange("p t (u h) -> p t u h", u=2), ACT.Exp).then_inc(exp_ready, 1)

            def one(g, b, i):
                weights(g, b)
                for n, (t0, k) in enumerate(G_GROUPS):
                    act.wait_ge(ohT_turn, g * len(G_GROUPS) + n + 1)
                    act.activation(ohT[:, b, t0 * 128:(t0 + k) * 128], turn[n % 2][0:WIN, 0:k * 128], ACT.Copy).then_inc(ohT_ready, 1)
                    act.wait_ge(ohT_ready, g * len(G_GROUPS) + n + 1)
                    act.sem_inc(turn_free, 1)
                messages(g, b, MT, MA, act_msg_ready)
                act.activation(mask[:, b, :], ohT[:, b, :], ACT.Copy, bias=-BIG, scale=BIG).then_inc(mask_ready, 1)
                window_out(g, b)
                for n, (t0, k) in enumerate(S_GROUPS):
                    act.wait_ge(sT_turn, g * len(S_GROUPS) + n + 1)
                    src = turn[(len(G_GROUPS) + n) % 2][0:SPLIT * H, 0:k * 64].bitcast(BF16)
                    act.activation(sT[:, t0 * 128:(t0 + k) * 128], src, ACT.Copy).then_inc(sT_ready, 1)
                    act.wait_ge(sT_ready, g * len(S_GROUPS) + n + 1)
                    act.sem_inc(turn_free, 1)
                messages(g, b, MA, CT, act_msg_ready)
                act.wait_ge(act_msg_ready, (g + 1) * (CT - MT))
                act.sem_inc(at["rows_free"], 1)
                scale_sums(g, b)

            def last(g, b, i):
                weights(g, b)
                messages(g, b, TT, CT, act_tail_ready)
                window_out(g, b)
                scale_sums(g, b)
                window_out(g + 1, 1 - b)
            pipeline(act, count, one, last)

            def h2(t, b, i):
                act.wait_ge(h2_var, t + 1)
                act.activation(rstd[:, b:b + 1], rstd[:, b:b + 1], ACT.Sqrt).then_inc(h2_std, 1)
                act.wait_ge(h2_shift, t + 1)
                act.wait_ge(s3["out_free"], t + 1)
                act.activation(nout[:, b, 0, :], x_sb[:, bass.ds(t, 1), :].rearrange("p a d -> p (a d)"), ACT.Relu,
                               bias=shift[:, b:b + 1], scale=rstd[:, b:b + 1]).then_inc(s3["out_ready"], 1)

            def h2_turned(t, b, i):
                act.activation(mx[0:1, 0, 0:1], ones[0:1, 0:1], ACT.Sqrt).then_inc(table_in, 1)
                act.wait_ge(table_in, t + 1)
                turned(t, b, i, s3, 2)
            ahead(act, NW, 1, h2_turned, h2)

            def fin(t, b, i):
                for k in range(2):
                    act.wait_ge(s5["turn_ready"], t * 2 + k + 1)
                    act.activation(ncol[:, k, :, :], turn[k][:, 0:KC * WIN].rearrange("p (c n) -> p c n", c=KC), ACT.Copy).then_inc(s5["col_ready"], 1)
            pairs(act, NW, fin)

        @block.tensor
        def _(pe):
            for s in (s1, s3, s5):
                pe.sem_inc(s["row_free"], 2)
                pe.sem_inc(s["turn_free"], 2)
                pe.sem_inc(s["sum_free"], 2)
                pe.sem_inc(s["out_free"], 2)
            for s in (at, ag):
                pe.sem_inc(s["pk_free"], 2)
                pe.sem_inc(s["acc_free"], 1)
                pe.sem_inc(s["out_free"], 1)
            pe.sem_inc(at["out_free"], LAG)
            pe.sem_inc(at["rows_free"], 2)
            pe.sem_inc(ag["rows_free"], 4)
            pe.sem_inc(unit_free, 1)
            pe.sem_inc(q_free, 2)
            pe.sem_inc(turn_free, 2)
            pe.sem_inc(wide_free, 2)
            pe.wait_ge(consts, 2)

            def offsets(j):
                pe.wait_ge(cnt_ready, j + 1)
                pe.matmul(offp, before[:, :], cnt[:, :], start=True, stop=True)
                pe.matmul(totp, ones[0:EP, :], cnt[:, :], start=True, stop=True).then_inc(offs_ready, 1)

            def to_cols(t, b, s):
                pe.wait_ge(s["turn_free"], t + 1)
                for c in range(KC):
                    last = pe.transpose(turn[b][:, c * WIN:(c + 1) * WIN], nrow[:, b, c * 128:(c + 1) * 128], ident[0:WIN, 0:WIN])
                last.then_inc(s["turn_ready"], 1)

            def product(out, b, w, start=True, stop=True):
                for c in range(KC):
                    last = pe.matmul(out, ncol[:, b, c, :], w_sb[:, w, c, :], start=start and c == 0, stop=stop and c == KC - 1)
                return last

            offsets(0)
            pe.wait_ge(w_in, 32)

            def qk_cols(t, b, i):
                pe.wait_ge(s1["row_ready"], t + 1)
                to_cols(t, b, s1)

            def qk(t, b, i):
                pe.wait_ge(s1["col_ready"], t + 1)
                pe.wait_ge(s1["sum_free"], t + 1)
                product(wide[b][0:WIN, 0:D], b, 0)
                product(wide[b][0:WIN, D:2 * D], b, 1).then_inc(s1["sum_ready"], 1)
            ahead(pe, NW, 1, qk_cols, qk)
            offsets(1)

            count = chunk_count_after(pe, 0)

            def add_messages(g, b, t, tail=False):
                if tail:
                    if t >= TT:
                        pe.wait_ge(act_tail_ready, t - TT + 1)
                    elif t % 4 == 0:
                        pe.wait_ge(tail_ready, t // 4 + 1)
                elif t >= MT:
                    pe.wait_ge(act_msg_ready, g * (CT - MT) + t - MT + 1)
                elif t % 4 == 0:
                    pe.wait_ge(msg_ready, g * len(M_GROUPS) + t // 4 + 1)
                if t == 0:
                    pe.wait_ge(at["acc_free"], g + 1)
                for u in range(2):
                    last = pe.matmul(halves[:, u, :], oh[:, 1 - b, t, :], sums_in[:, t, u, :], start=t == 0, stop=t == CT - 1)
                if t == CT - 1:
                    last.then_inc(at["acc_ready"], 1)

            def attend(g, b, i):
                pe.wait_ge(unit_free, g * UNITS + 1)
                pe.wait_ge(at["oh_ready"], g + 1)
                for n, (t0, k) in enumerate(G_GROUPS):
                    pe.wait_ge(turn_free, g * TURNS + n + 1)
                    for t in range(t0, t0 + k):
                        last = pe.transpose(turn[n % 2][0:WIN, (t - t0) * 128:(t - t0 + 1) * 128], oh[:, b, t, :], ident[:, :])
                    last.then_inc(ohT_turn, 1)
                todo = iter(range(CT))

                def sum_up(n):
                    for _ in range(SEG[n]):
                        add_messages(g, b, next(todo))

                pe.wait_ge(ohT_ready, g * len(G_GROUPS) + len(G_GROUPS))
                pe.wait_ge(q_in[b], i * 16 + 16)
                for n, (t0, k) in enumerate(Q_GROUPS):
                    pe.wait_ge(wide_free, g * len(Q_GROUPS) + n + 1)
                    for t in range(t0, t0 + k):
                        for part in range(SPLIT):
                            last = pe.matmul(wide[n % 2][:, (t - t0) * D:(t - t0 + 1) * D], ohT[:, b, t * 128:(t + 1) * 128],
                                             q_win[:, b, part, :], start=part == 0, stop=part == SPLIT - 1)
                    last.then_inc(q_ready, 1)
                    sum_up(n)
                pe.wait_ge(q_ready, (g + 1) * len(Q_GROUPS))
                pe.sem_inc(q_free, 1)

                def turn_scores(n):
                    t0, k = S_GROUPS[n]
                    pe.wait_ge(parts_ready, g * 2 + min(n, 1) + 1)
                    m = len(G_GROUPS) + n
                    pe.wait_ge(turn_free, g * TURNS + m + 1)
                    bank = turn[m % 2][0:SPLIT * H, :].bitcast(BF16)
                    for t in range(t0, t0 + k):
                        last = pe.transpose(bank[:, (t - t0) * 128:(t - t0 + 1) * 128], parts[:, t, :], identb[:, :])
                    last.then_inc(sT_turn, 1)
                turn_scores(0)
                sum_up(len(Q_GROUPS))
                pe.wait_ge(wide_free, (g + 1) * len(Q_GROUPS) + 2)
                for u in range(UNITS):
                    if u == 0:
                        pe.wait_ge(sT_ready, g * len(S_GROUPS) + 1)
                    if u == 2:
                        turn_scores(1)
                        turn_scores(2)
                        sum_up(len(Q_GROUPS) + 1)
                        pe.wait_ge(sT_ready, g * len(S_GROUPS) + len(S_GROUPS))
                    if u > 2:
                        pe.wait_ge(unit_free, g * UNITS + u - 1)
                    out = wide[u % 3][0:WIN, :]
                    if u < 2 * H:
                        half = u // H
                        for c in range(2):
                            last = pe.matmul(out[:, c * 512:(c + 1) * 512], sel[:, u % H, :],
                                             sT[:, half * HALF + c * 512:half * HALF + (c + 1) * 512], start=True, stop=True)
                    else:
                        for h in range(H):
                            last = pe.matmul(out[:, h * 128:(h + 1) * 128], sel[:, h, :], sT[:, 2 * HALF:CAP], start=True, stop=True)
                    last.then_inc(unit_ready, 1)
                    if u == UNITS - 1:
                        sum_up(len(Q_GROUPS) + 2)
                pe.wait_ge(m_ready, g + 1)
                for t in range(CT):
                    for part in range(SPLIT):
                        last = pe.matmul(mexp[:, t, :], ohT[:, b, t * 128:(t + 1) * 128], m_parts[:, part, :],
                                         start=part == 0, stop=part == SPLIT - 1)
                last.then_inc(mexp_ready, 1)

            def attend_last(g, b, i):
                for t in range(CT):
                    add_messages(g, b, t, True)
                pe.wait_ge(q_in[b], i * 16 + 16)
            pipeline(pe, count, attend, attend_last)

            pe.wait_ge(w_in, 64)

            def wo_cols(t, b, i):
                pe.wait_ge(load3[b], i * 32 + 32)
                to_cols(t, b, s3)

            def wo(t, b, i):
                pe.wait_ge(s3["col_ready"], t + 1)
                pe.sem_inc(s3["row_free"], 1)
                pe.wait_ge(s3["sum_free"], t + 1)
                product(wide[b][0:WIN, 0:D], b, 0).then_inc(s3["sum_ready"], 1)
            ahead(pe, NW, 1, wo_cols, wo)

            count1 = chunk_count_after(pe, 1)

            def agg(g, b, i):
                pe.wait_ge(ag["kept"], g + 1)
                pe.wait_ge(ag["rows_in"][b], (i + 1) * CT * 16)
                pe.wait_ge(ag["acc_free"], g + 1)
                pe.matmul(degp, oh_sum[:, b, :], ones[:, 0:1], start=True, stop=True)
                for t in range(CT):
                    last = pe.matmul(aggp, oh[:, b, t, :], rows[:, b, t, :], start=t == 0, stop=t == CT - 1)
                last.then_inc(ag["acc_ready"], 1)
                pe.wait_ge(ag["acc_ready"], g + 1)
                pe.sem_inc(ag["rows_free"], 2)
            chunks(pe, count1, agg)

            pe.wait_ge(w_in, 80)

            def fin_cols(t, b, i, k):
                if k == 0:
                    pe.wait_ge(load5[b], i * 32 + 32)
                src = nrow[:, b, :] if k == 0 else nout[:, b, 1, :]
                for c in range(KC):
                    last = pe.transpose(turn[k][:, c * WIN:(c + 1) * WIN], src[:, c * 128:(c + 1) * 128], ident[0:WIN, 0:WIN])
                last.then_inc(s5["turn_ready"], 1)

            def fin_product(t, b, k):
                if k == 0:
                    pe.wait_ge(s5["sum_free"], t + 1)
                pe.wait_ge(s5["col_ready"], t * 2 + k + 1)
                if k == 1:
                    pe.sem_inc(s5["row_free"], 1)
                last = product(wide[b][0:WIN, 0:D], k, 1 - k, start=k == 0, stop=k == 1)
                if k == 1:
                    last.then_inc(s5["sum_ready"], 1)

            def fin(t, b, i):
                for k in range(2):
                    fin_product(t, b, k)
                    fin_cols(t + 1, 1 - b, i + b, k)
            for k in range(2):
                fin_cols(0, 0, 0, k)
            pairs(pe, NW - 1, fin)
            for k in range(2):
                fin_product(NW - 1, 0, k)

        @block.vector
        def _(dve):
            steps = [0]

            def then(ins):
                steps[0] += 1
                ins.then_inc(step, 1)
                dve.wait_ge(step, steps[0])

            def moments(n):
                for t in range(NW):
                    last = dve.bn_aggr(mv[:, t, :], stats[:, t, :])
                then(last)
                dve.tensor_scalar(rstd[:, :], mv[:, :, 1], EPS, None, ALU.add).then_inc(var_ready, 1)
                dve.wait_ge(std_ready, n)
                then(dve.reciprocal(rstd[:, :], rstd[:, :]))
                dve.scalar_tensor_tensor(shift[:, :], mv[:, :, 0], -1.0, rstd[:, :], ALU.mult, ALU.mult).then_inc(norm_ready, 1)

            dve.memset(m_run[:, :], 0.0).then_inc(step, 1)
            dve.memset(den[:, :], 0.0).then_inc(step, 1)
            dve.memset(zero[:, :], 0.0).then_inc(step, 1)
            steps[0] = 3
            dve.wait_ge(step, 3)
            dve.wait_ge(consts, 2)
            dve.wait_ge(ends_in, 32)
            then(dve.tensor_copy(endf[:, :, :], ends[:, :, :]))
            for j in range(2):
                last = dve.scalar_tensor_tensor(ends[:, j, :], endf[:, j, :], float(2 ** SHIFT), endf[:, 1 - j, :], ALU.mult, ALU.add)
            then(last)

            tot, end, start, nch, cend, cst = (small[:, k, :] for k in range(1, 7))
            zrow = zero[:, 0:1].to_broadcast([128, NW])

            def places(j):
                win, win_b = tmpf[:, :], tmpb[:, :]
                then(dve.tensor_scalar(win, endf[:, j, :], -float(WIN // 2), 1.0 / WIN, ALU.add, ALU.mult))
                then(dve.tensor_scalar(win, win, ROUND, None, ALU.add))
                then(dve.tensor_scalar(win_b, win, -ROUND, None, ALU.add))
                for w in range(NW):
                    last = dve.tensor_scalar(hot[:, w * EI:(w + 1) * EI], win_b, float(w), None, ALU.is_equal)
                then(last)
                then(dve.tensor_tensor_scan(prefix, zero[0:EP, 0:1].to_broadcast([EP, NW * EI]), hot, 0.0, ALU.add, ALU.add))
                upto = prefix.rearrange("p (w i) -> p w i", w=NW)
                then(dve.tensor_copy(small[0:EP, 0, :], upto[:, :, EI - 1]))
                then(dve.tensor_copy(cnt[:, 0:1], small[0:EP, 0, 0:1]))
                dve.tensor_tensor(cnt[:, 1:NW], small[0:EP, 0, 1:NW], small[0:EP, 0, 0:NW - 1], ALU.subtract).then_inc(cnt_ready, 1)
                dve.wait_ge(offs_ready, j + 1)
                off = small[0:EP, 7, :]
                then(dve.tensor_copy(tot, totp))
                then(dve.tensor_tensor_scan(end, zrow, tot, 0.0, ALU.add, ALU.add))
                then(dve.tensor_tensor(start, end, tot, ALU.subtract))
                then(dve.tensor_tensor(off, offp, start[0:EP, :], ALU.add))
                then(dve.tensor_tensor(off, off, cnt[:, :], ALU.add))
                then(dve.tensor_tensor(off, off, small[0:EP, 0, :], ALU.subtract))
                then(dve.tensor_scalar(off, off, -1.0, None, ALU.add))
                for i0 in range(0, EI, EI // 2):
                    half = slice(i0, i0 + EI // 2)
                    for w in range(NW):
                        last = dve.scalar_tensor_tensor(upto[:, w, half], upto[:, w, half], off[:, w:w + 1], hot[:, w * EI:(w + 1) * EI][:, half], ALU.add, ALU.mult)
                    then(last)
                    then(dve.tensor_reduce(win[:, half], prefix.rearrange("p (w i) -> p i w", w=NW)[:, half, :], AX.X, ALU.add))
                    then(dve.tensor_copy(pos[:, j, half], win[:, half]))
                    dve.sem_inc(placed, 1)

            def chunk_tables(j):
                K = E // CAP + 1
                g3 = grid[:, 0:NW, 0:K]
                then(dve.tensor_tensor(g3, tot.unsqueeze(2).to_broadcast([128, NW, K]), limit[:, :].unsqueeze(1).to_broadcast([128, NW, K]), ALU.is_gt))
                then(dve.tensor_reduce(nch, g3, AX.X, ALU.add))
                then(dve.tensor_scalar(nch, nch, 1.0, None, ALU.max))
                then(dve.tensor_tensor_scan(cend, zrow, nch, 0.0, ALU.add, ALU.add))
                then(dve.tensor_tensor(cst, cend, nch, ALU.subtract))
                gs = iota[:, 0:GTAB].unsqueeze(2).to_broadcast([128, GTAB, NW])

                def each(v):
                    return v.unsqueeze(1).to_broadcast([128, GTAB, NW])
                then(dve.tensor_tensor(grid[:, :, :], each(cst), gs, ALU.is_le))
                then(dve.tensor_tensor(grid2[:, :, :], each(cend), gs, ALU.is_gt))
                then(dve.tensor_tensor(grid[:, :, :], grid[:, :, :], grid2[:, :, :], ALU.mult))
                base = small[:, 0, :]
                then(dve.scalar_tensor_tensor(base, cst, -float(CAP), start, ALU.mult, ALU.add))
                then(dve.tensor_tensor(grid2[:, :, :], grid[:, :, :], each(base), ALU.mult))
                then(dve.tensor_reduce(chunk_f[:, 0, :], grid2[:, :, :], AX.X, ALU.add))
                then(dve.scalar_tensor_tensor(chunk_f[:, 0, :], iota[:, 0:GTAB], float(CAP), chunk_f[:, 0, :], ALU.mult, ALU.add))
                then(dve.tensor_scalar(chunk_f[:, 0, :], chunk_f[:, 0, :], float(E), None, ALU.min))
                then(dve.tensor_tensor(grid2[:, :, :], grid[:, :, :], each(iota[:, 0:NW]), ALU.mult))
                then(dve.tensor_reduce(chunk_f[:, 1, :], grid2[:, :, :], AX.X, ALU.add))
                then(dve.tensor_scalar(chunk_f[:, 1, :], chunk_f[:, 1, :], float(WIN), None, ALU.mult))
                then(dve.tensor_tensor(grid2[:, :, :], each(cst), gs, ALU.is_equal))
                then(dve.tensor_reduce(chunk_f[:, 2, :], grid2[:, :, :], AX.X, ALU.add))
                then(dve.tensor_copy(chunk_f[:, 3, :], cend[:, NW - 1:NW].to_broadcast([128, GTAB])))
                for k, f in ((0, 0), (1, 1), (2, 3)):
                    then(dve.tensor_copy(chunk_i[0:1, j, k, LAG:GTAB + LAG], chunk_f[0:1, f, :]))
                then(dve.tensor_copy(chunk_p[0:1, j, :, 0], chunk_f[0:1, 1, :]))
                scale, plus = ((-2 * BIG, 0.0), (-1.0, 1.0))[j]
                then(dve.tensor_scalar(chunk_p[0:1, j, :, 1], chunk_f[0:1, 2, :], scale, plus, ALU.mult, ALU.add))
                dve.sem_inc(sort_ready, 1)

            places(0)
            chunk_tables(0)
            dve.wait_ge(x_in, 16)
            with dve.Fori(0, NW) as t:
                dve.bn_stats(stats[:, bass.ds(t, 1), :].rearrange("p a k -> p (a k)"),
                             x_sb[:, bass.ds(t, 1), :].rearrange("p a d -> p (a d)")).then_inc(s1["step"], 1)
            dve.wait_ge(s1["step"], NW)
            moments(1)

            dve.wait_ge(bias_in, 32)

            class Steps:
                def __init__(self, s, g, k):
                    self.s, self.first, self.k, self.n = s, g * k, k, 0

                def mark(self, ins):
                    self.n += 1
                    ins.then_inc(self.s, 1)
                    return self.n

                def seen(self, n):
                    hold(dve, "dve", self.s, self.first + n)

                def then(self, ins):
                    self.seen(self.mark(ins))

                def end(self):
                    assert self.n == self.k, (self.n, self.k)

            def exact_steps(part, value, rest):
                return (lambda: dve.tensor_copy(part(0), value),
                        lambda: dve.tensor_tensor(rest, value, part(0), ALU.subtract),
                        lambda: dve.tensor_copy(part(1), rest),
                        lambda: dve.tensor_tensor(rest, rest, part(1), ALU.subtract),
                        lambda: dve.tensor_copy(part(2), rest))

            def exact_parts(st, part, value, rest):
                for make in exact_steps(part, value, rest):
                    st.then(make())

            def qk(t, b, i):
                dve.wait_ge(s1["sum_ready"], t + 1)
                dve.wait_ge(s1["out_free"], t + 1)
                st = Steps(s1["q_step"], t, 7)
                q = nout[:, b, 0, :]
                st.mark(dve.tensor_tensor(q, wide[b][0:WIN, 0:D], bias[0][:, :], ALU.add))
                st.then(dve.tensor_tensor(nout[:, b, 1, :], wide[b][0:WIN, D:2 * D], bias[1][:, :], ALU.add))
                dve.sem_inc(s1["sum_free"], 1)
                exact_parts(st, lambda k: q_parts[:, b, k, :], q, q)
                st.end()
                dve.sem_inc(s1["out_ready"], 1)
            pairs(dve, NW, qk)
            places(1)
            chunk_tables(1)

            def decode(s, g, b, i):
                dve.wait_ge(s["pk_in"][b], i * 32 + 32)
                dve.tensor_scalar(idx[:, b, :], pk[:, b, :], 2 ** SHIFT - 1, None, ALU.bitwise_and).then_inc(s["idx_ready"], 1)
                dve.tensor_scalar(keyi[:, :], pk[:, b, :], SHIFT, None, ALU.logical_shift_right).then_inc(s["decode"], 1)
                dve.tensor_copy(first_chunk[:, b, :], par[:, b, 1:2]).then_inc(s["decode"], 1)
                dve.wait_ge(s["decode"], g * 3 + 2)
                dve.tensor_scalar(loc[:, b, :], keyi[:, :], par[:, b, 0:1], None, ALU.subtract).then_inc(s["decode"], 1)
                dve.wait_ge(s["decode"], g * 3 + 3)
                dve.wait_ge(s["idx_ready"], g + 1)
                dve.sem_inc(s["pk_free"], 1)

            def one_hot(s, g, b):
                dve.tensor_tensor(oh[:, b, :, :], iota[:, 0:WIN].unsqueeze(1).to_broadcast([128, CT, WIN]),
                                  loc[:, b, :].unsqueeze(2).to_broadcast([128, CT, WIN]), ALU.is_equal).then_inc(s["oh_ready"], 1)

            def by_head(v, n):
                return v.unsqueeze(1).to_broadcast([n, DH, H])

            dve.memset(rows[:, 1, :, :], 0.0).then_inc(step, 1)
            dve.memset(oh[:, 1, :, :], 0.0).then_inc(step, 1)
            dve.memset(res[:, :, :], 0.0).then_inc(step, 1)
            dve.memset(acc[:, :], 0.0).then_inc(step, 1)
            dve.memset(rden[:, :], 0.0).then_inc(step, 1)
            then(dve.memset(dif[:, :], 0.0))
            steps[0] += 5
            dve.wait_ge(step, steps[0])
            dve.sem_inc(res_ready, 1)
            dve.sem_inc(dif_ready, 1)
            dve.sem_inc(merged, 1)
            count = chunk_count(dve, 0)
            decode(at, 0, 0, 0)
            one_hot(at, 0, 0)

            def messages(g, b, groups, ready):
                dve.wait_ge(exp_ready, g + 1)
                for t0, k in groups:
                    weights = ex[:, t0:t0 + k, :].unsqueeze(2).to_broadcast([128, k, DH // 2, H])
                    for u in range(2):
                        out, k_rows = (v.rearrange("p t (d h) -> p t d h", h=H) for v in (msgs[:, t0:t0 + k, u, :], rows[:, 1 - b, t0:t0 + k, u * HD:(u + 1) * HD]))
                        last = dve.tensor_tensor(out, k_rows, weights, ALU.mult)
                    last.then_inc(ready, 1)

            MERGE = 5

            def in_halves(v):
                return v[:, :].rearrange("p (u c) -> p u c", u=2)

            def merge(st, g, b):
                dve.wait_ge(alpha_ready, g + 1)
                st.then(dve.tensor_tensor(den[:, :], den[:, :], alpha[:, 1 - b, :], ALU.mult))
                dve.wait_ge(at["acc_ready"], g + 1)
                st.mark(dve.tensor_tensor(in_halves(den), in_halves(den), denp, ALU.add))
                dve.wait_ge(acc_scaled, g + 1)
                st.mark(dve.tensor_tensor(in_halves(acc), in_halves(acc), accp, ALU.add))
                st.seen(st.n - 1)
                st.then(dve.tensor_scalar(rden[:, :], den[:, :], 1e-30, None, ALU.max))
                dve.sem_inc(at["acc_free"], 1)
                st.then(dve.reciprocal(rden[:, :], rden[:, :]))
                dve.sem_inc(merged, 1)

            def attend(g, b, i):
                st = Steps(at["step"], g, 2 * len(Q_GROUPS) + 10 + UNITS + 1 + 1 + 5 + 1 + MERGE)
                messages(g, b, M_GROUPS, msg_ready)
                hold(dve, "dve", msg_ready, g * len(M_GROUPS) + len(M_GROUPS))
                dve.sem_inc(at["rows_free"], 1)
                decode(at, g + 1, 1 - b, i + b)
                dve.wait_ge(at["rows_in"][b], (i + 1) * CT * 16)
                made, summed, split = [], [], []
                HT = HALF // 128

                def score_parts(t0, t1):
                    return (lambda k: parts[:, t0:t1, k * H:(k + 1) * H]), sc[:, t0:t1, :], res[:, t0:t1, :]
                first_half = exact_steps(*score_parts(0, HT))

                def split_some(n):
                    if n > HT // 2 and len(split) < len(first_half):
                        st.seen(split[-1] if split else summed[HT // 2 - 1])
                        split.append(st.mark(first_half[len(split)]()))

                for n in range(len(Q_GROUPS) + 1):
                    if n < len(Q_GROUPS):
                        t0, k = Q_GROUPS[n]
                        dve.wait_ge(q_ready, g * len(Q_GROUPS) + n + 1)
                        if n >= 3:
                            st.seen(summed[n - 3])
                        made.append(st.mark(dve.tensor_tensor(prod[:, n % 3, 0:k * D], wide[n % 2][:, 0:k * D],
                                                              rows[:, b, t0:t0 + k, :].rearrange("p t d -> p (t d)"), ALU.mult)))
                    split_some(n)
                    if n > 0:
                        t0, k = Q_GROUPS[n - 1]
                        st.seen(made[n - 1])
                        dve.sem_inc(wide_free, 1)
                        summed.append(st.mark(dve.tensor_reduce(sc[:, t0:t0 + k, :], prod[:, (n - 1) % 3, 0:k * D].rearrange("p (t d h) -> p t h d", t=k, h=H),
                                                                AX.X, ALU.add)))
                    split_some(n)
                    if n == len(Q_GROUPS) - 1:
                        st.seen(split[-1])
                        dve.sem_inc(parts_ready, 1)
                st.seen(summed[-1])
                exact_parts(st, *score_parts(HT, CT))
                dve.sem_inc(parts_ready, 1)
                dve.wait_ge(mask_ready, g + 1)
                found = []
                for u in range(UNITS):
                    hold(dve, "dve", unit_ready, g * UNITS + u + 1)
                    unit = wide[u % 3][0:WIN, :]
                    if u < 2 * H:
                        found.append(st.mark(dve.tensor_tensor_reduce(
                            out=junk[0:WIN, u % 2, :], in0=unit, in1=mask[:, b, (u // H) * HALF:(u // H + 1) * HALF], scale=1.0,
                            scalar=-3 * BIG, op0=ALU.add, op1=ALU.max, accum_out=mx[:, u % H, u // H:u // H + 1])))
                    else:
                        for h in range(H):
                            last = dve.tensor_tensor_reduce(
                                out=junk[0:WIN, u % 2, h * 128:(h + 1) * 128], in0=unit[:, h * 128:(h + 1) * 128], in1=mask[:, b, 2 * HALF:CAP], scale=1.0,
                                scalar=-3 * BIG, op0=ALU.add, op1=ALU.max, accum_out=mx[:, h, 2:3])
                        found.append(st.mark(last))
                    if u > 0:
                        st.seen(found[u - 1])
                        dve.sem_inc(unit_free, 1)
                st.seen(found[-1])
                dve.sem_inc(unit_free, 1)
                st.then(dve.tensor_reduce(dif[:, :], mx[:, :, :], AX.X, ALU.max))
                st.then(dve.scalar_tensor_tensor(m_new[:, :], m_run[:, :], first_chunk[0:WIN, b, :], dif[:, :], ALU.add, ALU.max))
                exact_parts(st, lambda k: m_parts[:, k, :], m_new[:, :], m_res[:, :])
                dve.sem_inc(m_ready, 1)
                st.then(dve.scalar_tensor_tensor(dif[:, :], m_run[:, :], first_chunk[0:WIN, b, :], m_new[:, :], ALU.add, ALU.subtract))
                dve.sem_inc(dif_ready, 1)
                dve.tensor_copy(m_run[:, :], m_new[:, :]).then_inc(at["kept"], 1)
                dve.wait_ge(at["acc_ready"], g + 1)
                one_hot(at, g + 1, 1 - b)
                dve.wait_ge(at["kept"], g + 1)
                dve.wait_ge(mexp_ready, g + 1)
                dve.tensor_tensor(res[:, :, :], sc[:, :, :], mexp, ALU.subtract).then_inc(res_ready, 1)
                merge(st, g, b)
                st.end()

            def attend_last(g, b, i):
                st = Steps(at["last_step"], 0, MERGE)
                messages(g, b, [(t, 4) for t in range(0, TT, 4)], tail_ready)
                merge(st, g, b)
                st.end()
            pipeline(dve, count, attend, attend_last)

            count1 = chunk_count(dve, 1)

            def sum_hot(g, b):
                one_hot(ag, g, b)
                dve.wait_ge(ag["oh_ready"], g + 1)
                dve.tensor_reduce(oh_sum[:, b, :], oh[:, b, :, :].rearrange("p t n -> p n t"), AX.X, ALU.add).then_inc(ag["kept"], 1)
            for b in range(2):
                decode(ag, b, b, 0)

            dve.wait_ge(bias_in, 48)

            def wo_sum(t, b):
                dve.wait_ge(s3["sum_ready"], t + 1)
                dve.tensor_tensor(win_out[:, :], wide[b][0:WIN, 0:D], bias[0][:, :], ALU.add).then_inc(s3["q_step"], 1)

            def wo_stats(t, b):
                xt = x_sb[:, bass.ds(t, 1), :].rearrange("p a d -> p (a d)")
                dve.wait_ge(s3["q_step"], t + 1)
                dve.sem_inc(s3["sum_free"], 1)
                dve.tensor_tensor(xt, xt, win_out[:, :], ALU.add).then_inc(s3["step"], 1)
                hold(dve, "dve", s3["step"], t * 4 + 1)
                dve.bn_stats(stats[:, b, :], xt).then_inc(s3["step"], 1)
                hold(dve, "dve", s3["step"], t * 4 + 2)
                dve.bn_aggr(mv[:, b, :], stats[:, b, :]).then_inc(s3["step"], 1)
                dve.wait_ge(s3["step"], t * 4 + 3)
                dve.wait_ge(s3["out_free"], t + 1)
                dve.tensor_scalar(rstd[:, b:b + 1], mv[:, b, 1:2], EPS, None, ALU.add).then_inc(s3["step"], 1)
                dve.wait_ge(s3["step"], t * 4 + 4)
                dve.sem_inc(h2_var, 1)

            def wo_norm(t, b):
                dve.wait_ge(h2_std, t + 1)
                dve.reciprocal(rstd[:, b:b + 1], rstd[:, b:b + 1]).then_inc(h2_rstd, 1)
                dve.wait_ge(h2_rstd, t + 1)
                dve.scalar_tensor_tensor(shift[:, b:b + 1], mv[:, b, 0:1], -1.0, rstd[:, b:b + 1], ALU.mult, ALU.mult).then_inc(h2_shift, 1)

            def wo(t, b, i):
                wo_sum(t, b)
                wo_stats(t, b)
                wo_norm(t, b)
            pairs(dve, NW, wo)

            for b in range(2):
                sum_hot(b, b)
            then(dve.memset(acc[:, :], 0.0))
            then(dve.memset(den[:, 0:1], 0.0))

            def agg(g, b, i):
                st = Steps(ag["step"], g, 5)
                keep = first_chunk[0:WIN, b, :]
                dve.wait_ge(ag["acc_ready"], g + 1)
                st.mark(dve.scalar_tensor_tensor(acc[:, :], acc[:, :], keep, aggp, ALU.mult, ALU.add))
                st.then(dve.scalar_tensor_tensor(den[:, 0:1], den[:, 0:1], keep, degp, ALU.mult, ALU.add))
                dve.sem_inc(ag["acc_free"], 1)
                with dve.If(g + 2 < count1):
                    decode(ag, g + 2, b, i + 1)
                    sum_hot(g + 2, b)
                st.then(dve.tensor_scalar(rden[:, 0:1], den[:, 0:1], 1.0, None, ALU.max))
                st.then(dve.reciprocal(rden[:, 0:1], rden[:, 0:1]))
                dve.wait_ge(ag["out_free"], g + 1)
                st.then(dve.tensor_scalar(win_out[:, :], acc[:, :], rden[:, 0:1], None, ALU.mult))
                dve.sem_inc(ag["out_ready"], 1)
                st.end()
            chunks(dve, count1, agg)

            dve.wait_ge(bias_in, 80)
            then(dve.tensor_tensor(bias[0][:, :], bias[0][:, :], bias[1][:, :], ALU.add))

            def fin(t, b, i):
                dve.wait_ge(s5["sum_ready"], t + 1)
                dve.tensor_tensor(win_out[:, :], wide[b][0:WIN, 0:D], bias[0][:, :], ALU.add).then_inc(s5["step"], 1)
                dve.wait_ge(s5["step"], t + 1)
                dve.sem_inc(s5["sum_free"], 1)
                dve.wait_ge(s5["out_free"], t + 1)
                dve.tensor_tensor(nout[:, b, 0, :], win_out[:, :], x_sb[:, bass.ds(t, 1), :].rearrange("p a d -> p (a d)"), ALU.add).then_inc(s5["out_ready"], 1)
                hold(dve, "dve", s5["out_ready"], t + 1)
            pairs(dve, NW, fin)


def kernel(x, src, dst, L0_gnn_Wq, L0_gnn_bq, L0_gnn_Wk, L0_gnn_bk, L0_gnn_Wo, L0_gnn_bo,
           L1_gnn_W1, L1_gnn_b1, L1_gnn_W2, L1_gnn_b2):
    import numpy as np
    import concourse.bacc as bacc
    from concourse import mybir
    from concourse.bass_utils import run_bass_kernel_spmd

    nc = bacc.Bacc("TRN2", target_bir_lowering=False, num_devices=1)
    arrays = {
        "x": x, "src": src, "dst": dst, "Wq": L0_gnn_Wq, "bq": L0_gnn_bq, "Wk": L0_gnn_Wk, "bk": L0_gnn_bk,
        "Wo": L0_gnn_Wo, "bo": L0_gnn_bo, "W1T": np.asarray(L1_gnn_W1).T, "b1": L1_gnn_b1,
        "W2T": np.asarray(L1_gnn_W2).T, "b2": L1_gnn_b2,
    }
    arrays = {n: np.ascontiguousarray(a) for n, a in arrays.items()}
    io = {n: nc.dram_tensor(n, a.shape, mybir.dt.from_np(a.dtype), kind="ExternalInput").ap() for n, a in arrays.items()}
    io["out"] = nc.dram_tensor("out", arrays["x"].shape, mybir.dt.float32, kind="ExternalOutput").ap()
    build(nc, io)
    r = run_bass_kernel_spmd(nc, [arrays], core_ids=[0])
    return r.results[0]["out"]
```
